# Optimizing a Trainium2 kernel written in Bass

```python
import numpy as np
import jax
import jax.numpy as jnp

def _softmax(x, axis=-1):
    return jax.nn.softmax(x, axis=axis)

def _gelu(x):
    return jax.nn.gelu(x, approximate=True)

def _silu(x):
    return jax.nn.silu(x)

def _sigmoid(x):
    return jax.nn.sigmoid(x)

def _layernorm(x, axis=-1, eps=1e-05):
    m = jnp.mean(x, axis=axis, keepdims=True)
    v = jnp.var(x, axis=axis, keepdims=True)
    return (x - m) / jnp.sqrt(v + eps)

def _scatter_add(tgt, idx, src, axis=0):
    return tgt.at[idx].add(src)

def _segment_sum(src, seg, n):
    return jax.ops.segment_sum(src, seg, n)
kernel_name = 'mk_adj_resnorm_d4_adj_r2_daed04'

def setup_inputs(seed: int=0):
    np.random.seed(seed)
    _w = jnp.asarray

    def _rec_inputs():
        import jax
        import jax.numpy as jnp
        _gk = jax.random.key(seed)
        x = -9.806e-05 + 1 * jax.random.normal(jax.random.fold_in(_gk, 1), (4096, 64), jnp.float32)
        _w = (1.0 + jnp.arange(4096, dtype=jnp.float32)) ** (-0.5)
        _w = _w / _w.mean()
        _pij = jnp.clip(0.000488281 * _w[:, None] * _w[None, :], 0.0, 1.0)
        _a = jax.random.uniform(jax.random.fold_in(_gk, 2), (4096, 4096)) < _pij
        adj = _a.astype(jnp.int32)
        return (x, adj)
    x, adj = _rec_inputs()

    def _L0_gnn_setup():
        import jax, jax.numpy as jnp
        import numpy as np
        ALPHA = 0.2
        NEG_BIG = jnp.float32(-9000000000000000.0)
        key = jax.random.key(seed)
        k1, k2, k3, k4 = jax.random.split(key, 4)
        N, F_IN, F_OUT = (4096, 64, 64)
        inputs = jax.random.normal(k1, (N, F_IN), dtype=jnp.float32)
        adj = jax.random.randint(k2, (N, N), 0, 2, dtype=jnp.int32)
        gain = 1.414
        lim_w = gain * np.sqrt(6.0 / (F_IN + F_OUT))
        W = jax.random.uniform(k3, (F_IN, F_OUT), dtype=jnp.float32, minval=-lim_w, maxval=lim_w)
        lim_a = gain * np.sqrt(6.0 / (2 * F_OUT + 1))
        a = jax.random.uniform(k4, (2 * F_OUT, 1), dtype=jnp.float32, minval=-lim_a, maxval=lim_a)
        return {'inputs': inputs, 'adj': adj, 'W': W, 'a': a}
    _L0_gnn_all = _L0_gnn_setup()
    _L0_gnn_in = {k: v for k, v in _L0_gnn_all.items() if k in ('W', 'a')}
    del _L0_gnn_all

    def _L1_gnn_setup():
        import jax, jax.numpy as jnp
        import numpy as np
        N = 6144
        IN_C = 64
        OUT_C = 64
        NEG_INF = -1000000000.0
        key = jax.random.key(seed)
        k1, k2, k3, k4 = jax.random.split(key, 4)
        x = jax.random.normal(k1, (N, IN_C), dtype=jnp.float32)
        edge_index = jax.random.randint(k2, (N, N), 0, 2, dtype=jnp.int32)
        weight_w = jax.random.normal(k3, (IN_C, OUT_C), dtype=jnp.float32) * (1.0 / np.sqrt(IN_C))
        weight_a = jax.random.normal(k4, (2 * OUT_C, 1), dtype=jnp.float32) * (1.0 / np.sqrt(OUT_C))
        bias = jnp.zeros((OUT_C,), dtype=jnp.float32)
        return {'x': x, 'edge_index': edge_index, 'weight_w': weight_w, 'weight_a': weight_a, 'bias': bias}
    _L1_gnn_all = _L1_gnn_setup()
    _L1_gnn_in = {k: v for k, v in _L1_gnn_all.items() if k in ('weight_w', 'weight_a', 'bias')}
    del _L1_gnn_all

    def _L2_gnn_setup():
        import jax, jax.numpy as jnp
        import numpy as np
        ALPHA = 0.2
        NEG_INF = -9000000000000000.0
        key = jax.random.key(seed)
        k1, k2, k3, k4 = jax.random.split(key, 4)
        N, F_IN, F_OUT = (512, 64, 64)
        h = jax.random.normal(k1, (N, F_IN), dtype=jnp.float32)
        adj = jax.random.randint(k2, (N, N), 0, 2, dtype=jnp.int32)
        lim_W = 1.414 * np.sqrt(6.0 / (F_IN + F_OUT))
        W = jax.random.uniform(k3, (F_IN, F_OUT), minval=-lim_W, maxval=lim_W, dtype=jnp.float32)
        lim_a = 1.414 * np.sqrt(6.0 / (2 * F_OUT + 1))
        a = jax.random.uniform(k4, (2 * F_OUT, 1), minval=-lim_a, maxval=lim_a, dtype=jnp.float32)
        return {'h': h, 'adj': adj, 'W': W, 'a': a}
    _L2_gnn_all = _L2_gnn_setup()
    _L2_gnn_in = {k: v for k, v in _L2_gnn_all.items() if k in ('W', 'a')}
    del _L2_gnn_all

    def _L3_gnn_setup():
        import jax, jax.numpy as jnp
        import numpy as np
        N = 4096
        F_IN = 64
        F_OUT = 64
        NEG_SLOPE = 0.01
        MASK_FILL = -1000000000000.0
        key = jax.random.key(seed)
        k1, k2, k3, k4 = jax.random.split(key, 4)
        x = jax.random.normal(k1, (N, F_IN), dtype=jnp.float32)
        adj_matrix = jax.random.randint(k2, (N, N), 0, 2, dtype=jnp.int32)
        W = jax.random.normal(k3, (F_IN, F_OUT), dtype=jnp.float32) * (1.0 / np.sqrt(F_IN))
        a = jax.random.normal(k4, (2 * F_IN, 1), dtype=jnp.float32) * (1.0 / np.sqrt(2 * F_IN))
        return {'x': x, 'adj_matrix': adj_matrix, 'W': W, 'a': a}
    _L3_gnn_all = _L3_gnn_setup()
    _L3_gnn_in = {k: v for k, v in _L3_gnn_all.items() if k in ('W', 'a')}
    del _L3_gnn_all
    return {'x': x, 'adj': adj, 'L0_gnn_W': _L0_gnn_in['W'], 'L0_gnn_a': _L0_gnn_in['a'], 'L1_gnn_weight_w': _L1_gnn_in['weight_w'], 'L1_gnn_weight_a': _L1_gnn_in['weight_a'], 'L1_gnn_bias': _L1_gnn_in['bias'], 'L2_gnn_W': _L2_gnn_in['W'], 'L2_gnn_a': _L2_gnn_in['a'], 'L3_gnn_W': _L3_gnn_in['W'], 'L3_gnn_a': _L3_gnn_in['a']}

def reference(x, adj, L0_gnn_W, L0_gnn_a, L1_gnn_weight_w, L1_gnn_weight_a, L1_gnn_bias, L2_gnn_W, L2_gnn_a, L3_gnn_W, L3_gnn_a):
    import jax
    import jax.numpy as jnp

    def _L0_gnn_ref(inputs, adj, W, a):
        import jax, jax.numpy as jnp
        import numpy as np
        ALPHA = 0.2
        NEG_BIG = jnp.float32(-9000000000000000.0)
        Wh = inputs @ W
        F_out = W.shape[1]
        a_src = a[:F_out, 0]
        a_dst = a[F_out:, 0]
        e = (Wh @ a_src)[:, None] + (Wh @ a_dst)[None, :]
        e = jnp.where(e > 0, e, ALPHA * e)
        scores = jnp.where(adj > 0, e, NEG_BIG)
        attention = jax.nn.softmax(scores, axis=1)
        h_prime = attention @ Wh
        return jax.nn.elu(h_prime)

    def _L1_gnn_ref(x, edge_index, weight_w, weight_a, bias):
        import jax, jax.numpy as jnp
        import numpy as np
        N = 6144
        IN_C = 64
        OUT_C = 64
        NEG_INF = -1000000000.0
        wh = x @ weight_w
        a_src = weight_a[:OUT_C, 0]
        a_dst = weight_a[OUT_C:, 0]
        e = (wh @ a_src)[:, None] + (wh @ a_dst)[None, :]
        e = jax.nn.leaky_relu(e, negative_slope=0.01)
        scores = jnp.where(edge_index > 0, e, NEG_INF)
        attention = jax.nn.softmax(scores, axis=1)
        out = attention @ wh
        return out + bias

    def _L2_gnn_ref(h, adj, W, a):
        import jax, jax.numpy as jnp
        import numpy as np
        ALPHA = 0.2
        NEG_INF = -9000000000000000.0
        F_OUT = W.shape[1]
        Wh = h @ W
        a1, a2 = (a[:F_OUT, 0], a[F_OUT:, 0])
        e = (Wh @ a1)[:, None] + (Wh @ a2)[None, :]
        e = jax.nn.leaky_relu(e, negative_slope=ALPHA)
        scores = jnp.where(adj > 0, e, jnp.float32(NEG_INF))
        attention = jax.nn.softmax(scores, axis=1)
        h_prime = attention @ Wh
        return jax.nn.elu(h_prime)

    def _L3_gnn_ref(x, adj_matrix, W, a):
        import jax, jax.numpy as jnp
        import numpy as np
        N = 4096
        F_IN = 64
        F_OUT = 64
        NEG_SLOPE = 0.01
        MASK_FILL = -1000000000000.0
        h = x @ W
        a1 = a[:F_OUT, 0]
        a2 = a[F_OUT:, 0]
        f1 = h @ a1
        f2 = h @ a2
        e = jax.nn.leaky_relu(f1[:, None] + f2[None, :], NEG_SLOPE)
        e = jnp.where(adj_matrix > 0, e, MASK_FILL)
        attention = jax.nn.softmax(e, axis=1)
        h_prime = attention @ h
        return jax.nn.elu(h_prime)
    x = _layernorm(x + _L0_gnn_ref(x, adj, L0_gnn_W, L0_gnn_a), axis=-1)
    x = _layernorm(x + _L1_gnn_ref(x, adj, L1_gnn_weight_w, L1_gnn_weight_a, L1_gnn_bias), axis=-1)
    x = _layernorm(x + _L2_gnn_ref(x, adj, L2_gnn_W, L2_gnn_a), axis=-1)
    x = _layernorm(x + _L3_gnn_ref(x, adj, L3_gnn_W, L3_gnn_a), axis=-1)
    return x

_drawn_inputs = setup_inputs


def setup_inputs(seed=0):
    import zlib

    import numpy as np

    out = dict(_drawn_inputs(seed))
    spreads = {'L1_gnn_bias': (0.0, 0.1)}
    factors = {}
    for name, (base, spread) in spreads.items():
        noise = np.random.default_rng([zlib.crc32(name.encode()), seed]).standard_normal(out[name].shape)
        drawn = base * np.exp(spread * noise) if base else spread * noise
        out[name] = jnp.asarray(drawn.astype(out[name].dtype))
    for name, factor in factors.items():
        out[name] = (out[name] * factor).astype(out[name].dtype)
    return out
```

```python
from contextlib import ExitStack

import numpy as np

import concourse.bass as bass
from concourse import mybir

ALU = mybir.AluOpType
ACT = mybir.ActivationFunctionType
AX = mybir.AxisListType.X
F32 = mybir.dt.float32
F16 = mybir.dt.float16
BF16 = mybir.dt.bfloat16
I32 = mybir.dt.int32

P = 128
N = 4096
F = 64
TILES = N // P
LAYERS = 4
ALPHA = [0.2, 0.01, 0.2, 0.01]
ELU = [True, False, True, True]
BIAS_LAYER = 1
EPS = 1e-5
MASKED = -1e30
FLOOR = -1e20

BITS = 16
WORDS = N // BITS
WORDS_C = P // BITS
TCOL = F
SCOL = F + 1
WX = F + 2

CHUNKS = [13, 6, 5, 4, 4] + [3] * 8 + [2] * 19
ROOM = [96, 24] + [16] * 18 + [8] * 12
BASE = [sum(CHUNKS[:k]) for k in range(TILES + 1)]
NCH = BASE[TILES]
MAXC = max(CHUNKS)
MAXR = max(ROOM)
CENTER = N // 2

GROUP = 4
GROUPS = TILES // GROUP
SEG = 4
SEGS = []
for _k in range(TILES):
    for _c in range(0, CHUNKS[_k], SEG):
        SEGS.append((_k, _c, min(SEG, CHUNKS[_k] - _c)))
NSEG = len(SEGS)
SEG0 = [min(q for q in range(NSEG) if SEGS[q][0] == k) for k in range(TILES)]
SEGN = [sum(1 for s in SEGS if s[0] == k) for k in range(TILES)]
YRING = max(SEGN) + 1


LAG_EPILOGUE, LAG_XT, LAG_WH = 2, 3, 4


def group_ended(k):
    return 0 <= k < TILES and k % GROUP == GROUP - 1


def slot_batches(k):
    per = 512 // (ROOM[k] + 1)
    return [(c, min(per, CHUNKS[k] - c)) for c in range(0, CHUNKS[k], per)]


BATCH0 = [sum(len(slot_batches(j)) for j in range(k)) for k in range(TILES + 1)]


def gat_kernel(nc, x_in, adj, adj_t, weights, avecs, bias, consts, out):
    with ExitStack() as ctx:
        def sb(name, shape, dt):
            return ctx.enter_context(nc.sbuf_tensor(name, shape, dt))

        def bank(name):
            return ctx.enter_context(nc.psum_tensor(name, [P, 512], F32))

        def sem(name):
            return ctx.enter_context(nc.semaphore(name))

        table = [nc.dram_tensor(f"table{l}", [N, WX], F32, kind="Internal").ap() for l in range(LAYERS)]

        ident = sb("ident", [P, P], F32)
        ones = sb("ones", [P, P], F32)
        before = sb("before", [P, P], BF16)
        packer = sb("packer", [P, WORDS_C + 1], BF16)
        before_f = sb("before_f", [P, P], F32)
        packer_f = sb("packer_f", [P, WORDS_C + 1], F32)
        word_base = sb("word_base", [P, WORDS], F32)
        slot_row = sb("slot_row", [P, MAXC * P], F32)
        slot_col = sb("slot_col", [P, MAXC], F32)
        room_row = sb("room_row", [P, MAXR], F32)
        bit_mask = sb("bit_mask", [P, BITS], I32)
        bit_next = sb("bit_next", [P, BITS], F32)
        wx = sb("wx", [F, LAYERS, WX], F32)
        wt = sb("wt", [F, F], F32)
        av = sb("av", [F, LAYERS, 2], F32)
        bias_sb = sb("bias_sb", [P, F], F32)

        x = sb("x", [P, TILES, F], F32)
        wh = sb("wh", [P, TILES, WX], F32)
        xt = sb("xt", [F, 2, GROUP * P], F32)
        sum_wh = sb("sum_wh", [P, F], F32)

        arena = sb("arena", [P, 4, N], I32)
        masks = arena[:, 3, :].bitcast(BF16).rearrange("p (b n) -> p b n", b=2)
        key = sb("key", [P, 2, WORDS], F32)
        top = sb("top", [P, MAXR], F32)
        topi = sb("topi", [P, MAXR], I32)
        word16 = sb("word16", [P, MAXR], I32)
        bitv = sb("bitv", [P, MAXR * BITS], I32)
        colv = sb("colv", [P, MAXR * BITS], F32)
        cand = sb("cand", [P, 2, MAXR * BITS], F32)
        nbr = sb("nbr", [P, MAXR], F32)
        nbrh = sb("nbrh", [P, MAXR + 1], F16)
        deg = sb("deg", [P, TILES], F32)
        degb = sb("degb", [P, 1], BF16)
        ends = sb("ends", [P, TILES], F32)
        begun = sb("begun", [P, MAXC * P], BF16)
        inrow = sb("inrow", [P, MAXC * P], BF16)
        penalty = sb("penalty", [P, NCH * P], BF16)
        rank = sb("rank", [P, MAXC], F32)
        pick = sb("pick", [P, 512], F32)
        picked = sb("picked", [P, MAXC], F32)
        index = sb("index", [P, NCH], I32)
        lonely = sb("lonely", [P, TILES], F32)
        over = sb("over", [P, 2, TILES], F32)
        over_sum = sb("over_sum", [P, 1], F32)
        limits = sb("limits", [P, 2, TILES], F32)
        flag = sb("flag", [1, 1], I32)

        xg = sb("xg", [P, NCH, WX], F32)
        score = sb("score", [P, YRING, SEG * P], F32)
        slots_t = sb("slots_t", [P, 2, SEG * P], F32)
        seg_max = sb("seg_max", [P, NSEG], F32)
        seg_sum = sb("seg_sum", [P, NSEG], F32)
        sloped_own = sb("sloped_own", [P, TILES], F32)
        row_max = sb("row_max", [P, TILES], F32)
        neg_max = sb("neg_max", [P, TILES], F32)
        den = sb("den", [P, GROUP], F32)
        num = sb("num", [P, GROUP, F], F32)
        res = sb("res", [P, GROUP, F], F32)
        low = sb("low", [P, GROUP, F], F32)
        elow = sb("elow", [P, GROUP, F], F32)
        stat = sb("stat", [P, GROUP], F32)
        var = sb("var", [P, GROUP], F32)
        rstd = sb("rstd", [P, GROUP], F32)

        banks = [bank(f"bank{i}") for i in range(8)]
        codes_ps = banks[0:2]
        turned_ps = banks[0:2]
        score_ps = banks[2:4]
        off_ps = banks[2]
        list_ps = banks[3]
        agg_ps = banks[4:6]
        xt_ps = banks[6]
        wh_ps = banks[7]

        loaded = sem("loaded")
        adj_loaded = [sem(f"adj_loaded{i}") for i in range(3)]
        wt_done = sem("wt_done")
        wt_copied = sem("wt_copied")
        wa_done = sem("wa_done")
        wx_copied = sem("wx_copied")
        dve = sem("dve")
        mask_made = sem("mask_made")
        codes_made = sem("codes_made")
        codes_read = sem("codes_read")
        deg_made = sem("deg_made")
        off_made = sem("off_made")
        slots_made = sem("slots_made")
        list_made = sem("list_made")
        list_read = sem("list_read")
        over_made = sem("over_made")
        over_summed = sem("over_summed")
        flag_made = sem("flag_made")

        x_made = sem("x_made")
        xt_made = sem("xt_made")
        xt_copied = sem("xt_copied")
        wh_made = sem("wh_made")
        wh_copied = sem("wh_copied")
        written = sem("written")
        gathered = [sem(f"gathered{k}") for k in range(TILES)]
        sum_made = sem("sum_made")
        sum_copied = sem("sum_copied")
        score_made = sem("score_made")
        slope_made = sem("slope_made")
        sloped = sem("sloped")
        masked = sem("masked")
        max_made = sem("max_made")
        exped = sem("exped")
        turned = sem("turned")
        turned_copied = sem("turned_copied")
        agg_made = sem("agg_made")
        agg_read = sem("agg_read")
        low_made = sem("low_made")
        elow_made = sem("elow_made")
        elu_in = sem("elu_in")
        var_made = sem("var_made")
        ln_made = sem("ln_made")
        rstd_made = sem("rstd_made")
        stored = sem("stored")

        d_proj = sem("d_proj")
        d_trow = sem("d_trow")
        d_trow_copied = sem("d_trow_copied")
        d_adj = sem("d_adj")
        d_pen = sem("d_pen")
        d_slope = sem("d_slope")
        d_z = sem("d_z")
        d_max = sem("d_max")
        d_exp = sem("d_exp")
        d_turned = sem("d_turned")
        d_turned_copied = sem("d_turned_copied")
        d_agg = sem("d_agg")
        d_low = sem("d_low")
        d_elow = sem("d_elow")
        d_var = sem("d_var")
        d_ln = sem("d_ln")
        d_rstd = sem("d_rstd")
        d_x = sem("d_x")
        d_dve = sem("d_dve")

        NLOAD = 11 + 2 * LAYERS
        block = ctx.enter_context(nc.Block())

        x_v = x_in.rearrange("(k p) f -> p k f", p=P)
        out_v = out.rearrange("(k p) f -> p k f", p=P)
        tab_v = [t.rearrange("(k p) f -> p k f", p=P) for t in table]

        def tcol_wide(ap):
            return ap.broadcast_to([P, P])

        @block.sync
        def _(sp):
            for dst, src in [(ident, "ident"), (ones, "ones"), (before_f, "before"), (packer_f, "packer"),
                             (word_base, "word_base"), (slot_row, "slot_row"),
                             (slot_col, "slot_col"), (room_row, "room_row"), (bit_mask, "bit_mask"),
                             (bit_next, "bit_next"), (limits, "limits")]:
                d = dst[:, :] if len(dst.shape) == 2 else dst[:, :, :].rearrange("p a b -> p (a b)")
                sp.dma_start(d, consts[src]).then_inc(loaded, 16)
            for l in range(LAYERS):
                sp.dma_start(wx[:, l, 0:F], weights[l]).then_inc(loaded, 16)
                sp.dma_start(av[:, l, :], avecs[l]).then_inc(loaded, 16)
            sp.dma_start(bias_sb[:, :], bias.rearrange("(o f) -> o f", o=1).broadcast_to([P, F])).then_inc(loaded, 16)
            sp.dma_start(x[:, :, :], x_v).then_inc(loaded, 16)
            for k in range(TILES):
                if k >= 3:
                    sp.wait_ge(mask_made, k - 2)
                sp.dma_start(arena[:, k % 3, :], adj_t[k]).then_inc(adj_loaded[k % 3], 16)
            for g in range(GROUPS):
                sp.wait_ge(wh_copied, g + 1)
                sp.dma_start(tab_v[0][:, g * GROUP:(g + 1) * GROUP, :],
                             wh[:, g * GROUP:(g + 1) * GROUP, :]).then_inc(written, 16)
            sp.wait_ge(flag_made, 1)
            over_flag = sp.value_load(flag[0:1, 0:1], min_val=0, max_val=1)
            with sp.If(over_flag == 0):
                for l in range(LAYERS):
                    for g in range(GROUPS):
                        if l < LAYERS - 1:
                            n = (l + 1) * GROUPS + g
                            sp.wait_ge(wh_copied, n + 1)
                            sp.dma_start(tab_v[l + 1][:, g * GROUP:(g + 1) * GROUP, :],
                                         wh[:, g * GROUP:(g + 1) * GROUP, :]).then_inc(written, 16)
                        else:
                            sp.wait_ge(x_made, l * GROUPS + g + 1)
                            sp.dma_start(out_v[:, g * GROUP:(g + 1) * GROUP, :],
                                         x[:, g * GROUP:(g + 1) * GROUP, :]).then_inc(stored, 16)
                sp.wait_ge(stored, 16 * GROUPS)
                sp.wait_ge(written, 16 * LAYERS * GROUPS)
            with sp.Else():
                for l in range(LAYERS):
                    with sp.Fori(0, TILES) as k:
                        sp.wait_ge(d_x, l * TILES + k + 1)
                        sp.dma_start(arena[:, 0, :], adj[bass.ts(k, P), :]).then_inc(d_adj, 16)
                sp.wait_ge(d_x, LAYERS * TILES + 1)
                sp.dma_start(out_v, x[:, :, :]).then_inc(stored, 16)
                sp.wait_ge(stored, 16)
                sp.wait_ge(written, 16 * GROUPS)

        @block.gpsimd
        def _(pool):
            pool.wait_ge(flag_made, 1)
            over_flag = pool.value_load(flag[0:1, 0:1], min_val=0, max_val=1)
            with pool.If(over_flag == 0):
                for l in range(LAYERS):
                    pool.wait_ge(written, 16 * (l + 1) * GROUPS)
                    for k in range(TILES):
                        if l > 0 and k % GROUP == 0:
                            pool.wait_ge(agg_made, (l - 1) * GROUPS + k // GROUP + 1)
                        for c in range(BASE[k], BASE[k + 1]):
                            pool.indirect_dma_start(
                                out=xg[:, c, :], out_offset=None, in_=table[l][:, :],
                                in_offset=bass.IndirectOffsetOnAxis(ap=index[:, c:c + 1], axis=0),
                            ).then_inc(gathered[k], 16)

        @block.tensor
        def _(pe):
            def project(n, g, l):
                if n >= 1:
                    pe.wait_ge(xt_copied, n)
                for j in range(GROUP):
                    t = nc.tensor.transpose(xt_ps[0:F, j * P:(j + 1) * P], x[:, g * GROUP + j, :], ident[:, :])
                t.then_inc(xt_made, 1)
                pe.wait_ge(xt_copied, n + 1)
                if n >= 1:
                    pe.wait_ge(wh_copied, n)
                for j in range(GROUP):
                    t = nc.tensor.matmul(wh_ps[:, j * WX:(j + 1) * WX], xt[:, n % 2, j * P:(j + 1) * P],
                                         wx[:, l, :], start=True, stop=True)
                t.then_inc(wh_made, 1)

            def sum_rows(l):
                pe.wait_ge(wh_copied, (l + 1) * GROUPS)
                for k in range(TILES):
                    t = nc.tensor.matmul(wh_ps[:, 0:F], ones[:, :], wh[:, k, 0:F],
                                         start=(k == 0), stop=(k == TILES - 1))
                t.then_inc(sum_made, 1)

            pe.wait_ge(loaded, 16 * (NLOAD + 2))
            for l in range(LAYERS):
                if l >= 1:
                    pe.wait_ge(wx_copied, l)
                nc.tensor.transpose(xt_ps[0:F, 0:F], wx[:, l, 0:F], ident[0:F, 0:F]).then_inc(wt_done, 1)
                pe.wait_ge(wt_copied, l + 1)
                nc.tensor.matmul(wh_ps[0:F, 0:2], wt[:, :], av[:, l, :], start=True, stop=True).then_inc(wa_done, 1)
            pe.wait_ge(wx_copied, LAYERS)
            for g in range(GROUPS):
                project(g, g, 0)

            def pack(k):
                pe.wait_ge(mask_made, k + 1)
                if k >= 2:
                    pe.wait_ge(codes_read, k - 1)
                for c in range(TILES):
                    t = nc.tensor.matmul(codes_ps[k % 2][:, c * (WORDS_C + 1):(c + 1) * (WORDS_C + 1)],
                                         masks[:, k % 2, c * P:(c + 1) * P], packer[:, :], start=True, stop=True)
                t.then_inc(codes_made, 1)

            def place(k):
                pe.wait_ge(deg_made, k + 1)
                nc.tensor.matmul(off_ps[:, 0:1], before[:, :], degb[:, :], start=True, stop=True).then_inc(off_made, 1)
                pe.wait_ge(slots_made, k + 1)
                w = ROOM[k] + 1
                for b, (c0, nb) in enumerate(slot_batches(k)):
                    n = BATCH0[k] + b
                    if n >= 1:
                        pe.wait_ge(list_read, n)
                    for c in range(nb):
                        t = nc.tensor.matmul(list_ps[:, c * w:(c + 1) * w], inrow[:, (c0 + c) * P:(c0 + c + 1) * P],
                                             nbrh[:, 0:w], start=True, stop=True)
                    t.then_inc(list_made, 1)

            pack(0)
            for k in range(TILES):
                if k + 1 < TILES:
                    pack(k + 1)
                place(k)
            pe.wait_ge(over_made, 1)
            nc.tensor.matmul(off_ps[:, 0:1], ones[:, :], over_sum[:, :], start=True, stop=True).then_inc(over_summed, 1)

            pe.wait_ge(flag_made, 1)
            over_flag = pe.value_load(flag[0:1, 0:1], min_val=0, max_val=1)
            with pe.If(over_flag == 0):
                def spread(l, q):
                    k, c0, m = SEGS[q]
                    n = l * NSEG + q
                    pe.wait_ge(gathered[k], 16 * CHUNKS[k] * (l + 1))
                    if n >= 2:
                        pe.wait_ge(masked, n - 1)
                    for c in range(m):
                        t = nc.tensor.transpose(score_ps[n % 2][:, c * P:(c + 1) * P],
                                                tcol_wide(xg[:, BASE[k] + c0 + c, TCOL:TCOL + 1]), ident[:, :])
                    t.then_inc(score_made, 1)

                def turn(l, q):
                    k, c0, m = SEGS[q]
                    n = l * NSEG + q
                    pe.wait_ge(exped, n + 1)
                    if n >= 2:
                        pe.wait_ge(turned_copied, n - 1)
                    for c in range(m):
                        t = nc.tensor.transpose(turned_ps[n % 2][:, c * P:(c + 1) * P],
                                                score[:, n % YRING, c * P:(c + 1) * P], ident[:, :])
                    t.then_inc(turned, 1)

                def aggregate(l, q):
                    k, c0, m = SEGS[q]
                    n = l * NSEG + q
                    g = k // GROUP
                    ng = l * GROUPS + g
                    if k % GROUP == 0 and c0 == 0 and ng >= 2:
                        pe.wait_ge(agg_read, ng - 1)
                    pe.wait_ge(turned_copied, n + 1)
                    for c in range(m):
                        t = nc.tensor.matmul(agg_ps[ng % 2][:, (k % GROUP) * F:(k % GROUP + 1) * F],
                                             slots_t[:, n % 2, c * P:(c + 1) * P],
                                             xg[:, BASE[k] + c0 + c, 0:F],
                                             start=(c0 + c == 0), stop=(c0 + c == CHUNKS[k] - 1))
                    if k % GROUP == GROUP - 1 and c0 + m == CHUNKS[k]:
                        t.then_inc(agg_made, 1)

                for l in range(LAYERS):
                    sum_rows(l)
                    order = []
                    for k in range(TILES + LAG_WH + 1):
                        if k < TILES:
                            order += [("s", SEG0[k] + i) for i in range(SEGN[k])]
                        if 1 <= k <= TILES:
                            for i in range(SEGN[k - 1]):
                                order += [("t", SEG0[k - 1] + i), ("a", SEG0[k - 1] + i)]
                        if l < LAYERS - 1 and group_ended(k - LAG_XT):
                            order.append(("p", (k - LAG_XT) // GROUP))
                    for what, i in order:
                        if what == "s":
                            spread(l, i)
                        elif what == "t":
                            turn(l, i)
                        elif what == "a":
                            aggregate(l, i)
                        else:
                            pe.wait_ge(x_made, l * GROUPS + i + 1)
                            if i == 0:
                                pe.wait_ge(sum_copied, l + 1)
                            project((l + 1) * GROUPS + i, i, l + 1)
            with pe.Else():
                for l in range(LAYERS):
                    if l > 0:
                        pe.wait_ge(d_x, l * TILES + 1)
                        for g in range(GROUPS):
                            project(l * GROUPS + g, g, l)
                    pe.wait_ge(wh_copied, (l + 1) * GROUPS)
                    for k in range(TILES):
                        n = l * TILES + k
                        if n >= 2:
                            pe.wait_ge(d_trow_copied, n - 1)
                        nc.tensor.transpose(banks[2 + n % 2][:, 0:P], tcol_wide(wh[:, k, TCOL:TCOL + 1]),
                                            ident[:, :]).then_inc(d_trow, 1)
                    with pe.Fori(0, TILES) as k:
                        pe.wait_ge(d_exp, l * TILES + k + 1)
                        p_f = arena[:, 2, :].bitcast(F32)
                        for c4 in range(TILES // 4):
                            for c in range(4):
                                t = nc.tensor.transpose(turned_ps[0][:, c * P:(c + 1) * P],
                                                        p_f[:, (4 * c4 + c) * P:(4 * c4 + c + 1) * P], ident[:, :])
                            t.then_inc(d_turned, 1)
                            pe.wait_ge(d_turned_copied, (l * TILES + k) * (TILES // 4) + c4 + 1)
                            for c in range(4):
                                t = nc.tensor.matmul(agg_ps[0][:, 0:F], slots_t[:, 0, c * P:(c + 1) * P],
                                                     wh[:, 4 * c4 + c, 0:F],
                                                     start=(c4 + c == 0), stop=(c4 == TILES // 4 - 1 and c == 3))
                            if c4 == TILES // 4 - 1:
                                t.then_inc(d_agg, 1)

        @block.scalar
        def _(act):
            def copy_xt(n):
                act.wait_ge(xt_made, n + 1)
                if n >= 2:
                    act.wait_ge(wh_made, n - 1)
                nc.scalar.copy(xt[:, n % 2, :], xt_ps[0:F, :]).then_inc(xt_copied, 1)

            def estimate_rstd(n, asked, logged, answered, count):
                act.wait_ge(asked, count)
                nc.scalar.activation(rstd[:, 0:n], var[:, 0:n], ACT.Ln).then_inc(logged, 1)
                act.wait_ge(logged, count)
                nc.scalar.activation(rstd[:, 0:n], rstd[:, 0:n], ACT.Exp, scale=-0.5).then_inc(answered, 1)

            nc.scalar.preload_act_table_set("natural_log_exp_and_others")
            for l in range(LAYERS):
                act.wait_ge(wt_done, l + 1)
                if l >= 1:
                    act.wait_ge(wa_done, l)
                nc.scalar.copy(wt[:, :], xt_ps[0:F, 0:F]).then_inc(wt_copied, 1)
            for g in range(GROUPS):
                copy_xt(g)

            act.wait_ge(flag_made, 1)
            over_flag = act.value_load(flag[0:1, 0:1], min_val=0, max_val=1)
            with act.If(over_flag == 0):
                def soften(l, q, step):
                    k, c0, m = SEGS[q]
                    n = l * NSEG + q
                    s = score[:, n % YRING, 0:m * P]
                    if step == 0:
                        act.wait_ge(score_made, n + 1)
                        if n >= YRING:
                            act.wait_ge(turned, n - YRING + 1)
                        if k % GROUP == 0 and c0 == 0:
                            act.wait_ge(slope_made, l * GROUPS + k // GROUP + 1)
                        nc.scalar.activation(s, score_ps[n % 2][:, 0:m * P], ACT.Identity, bias=sloped_own[:, k:k + 1],
                                             scale=ALPHA[l]).then_inc(sloped, 1)
                    else:
                        act.wait_ge(max_made, l * TILES + k + 1)
                        nc.scalar.activation(s, s, ACT.Exp, bias=neg_max[:, k:k + 1],
                                             accum_out=seg_sum[:, q:q + 1]).then_inc(exped, 1)

                def copy_turned(l, q):
                    k, c0, m = SEGS[q]
                    n = l * NSEG + q
                    act.wait_ge(turned, n + 1)
                    nc.scalar.copy(slots_t[:, n % 2, 0:m * P], turned_ps[n % 2][:, 0:m * P]).then_inc(turned_copied, 1)

                e = 0
                for l in range(LAYERS):
                    for k in range(TILES + LAG_WH + 1):
                        if k < TILES:
                            for i in range(SEGN[k]):
                                soften(l, SEG0[k] + i, 0)
                            for i in range(SEGN[k]):
                                soften(l, SEG0[k] + i, 1)
                        if 1 <= k <= TILES:
                            for i in range(SEGN[k - 1]):
                                copy_turned(l, SEG0[k - 1] + i)
                        if group_ended(k - LAG_EPILOGUE):
                            if ELU[l]:
                                e += 1
                                act.wait_ge(elu_in, e)
                                nc.scalar.activation(elow[:, :, :], low[:, :, :], ACT.Exp).then_inc(elow_made, 1)
                            estimate_rstd(GROUP, var_made, ln_made, rstd_made,
                                          l * GROUPS + (k - LAG_EPILOGUE) // GROUP + 1)
                        if l < LAYERS - 1 and group_ended(k - LAG_XT):
                            copy_xt((l + 1) * GROUPS + (k - LAG_XT) // GROUP)
            with act.Else():
                e = 0
                for l in range(LAYERS):
                    if l > 0:
                        for g in range(GROUPS):
                            copy_xt(l * GROUPS + g)
                    for k in range(TILES):
                        n = l * TILES + k
                        act.wait_ge(d_trow, n + 1)
                        nc.scalar.copy(arena[:, 3, k * P:(k + 1) * P].bitcast(F32),
                                       banks[2 + n % 2][:, 0:P]).then_inc(d_trow_copied, 1)
                    z = arena[:, 2, :].bitcast(F32)
                    act.wait_ge(d_trow_copied, (l + 1) * TILES)
                    act.wait_ge(d_slope, l + 1)
                    with act.Fori(0, TILES) as k:
                        act.wait_ge(d_x, l * TILES + k + 1)
                        nc.scalar.activation(z, arena[:, 3, :].bitcast(F32), ACT.Identity,
                                             bias=sloped_own[:, bass.ds(k, 1)], scale=ALPHA[l]).then_inc(d_z, 1)
                        act.wait_ge(d_max, l * TILES + k + 1)
                        nc.scalar.activation(z, arena[:, 1, :].bitcast(F32), ACT.Exp, bias=neg_max[:, 0:1],
                                             accum_out=seg_sum[:, 0:1]).then_inc(d_exp, 1)
                        for c4 in range(TILES // 4):
                            act.wait_ge(d_turned, (l * TILES + k) * (TILES // 4) + c4 + 1)
                            nc.scalar.copy(slots_t[:, 0, :], turned_ps[0][:, :]).then_inc(d_turned_copied, 1)
                        act.wait_ge(d_low, l * TILES + k + 1)
                        nc.scalar.activation(elow[:, 0, :], low[:, 0, :], ACT.Exp).then_inc(d_elow, 1)
                        estimate_rstd(1, d_var, d_ln, d_rstd, l * TILES + k + 1)

        @block.vector
        def _(v):
            steps = [0]

            def link(ins):
                steps[0] += 1
                ins.then_inc(dve, 1)
                v.wait_ge(dve, steps[0])

            def copy_wh(n, g):
                v.wait_ge(wh_made, n + 1)
                nc.vector.tensor_copy(wh[:, g * GROUP:(g + 1) * GROUP, :],
                                      wh_ps[:, 0:GROUP * WX].rearrange("p (j f) -> p j f", j=GROUP)).then_inc(wh_copied, 1)

            v.wait_ge(loaded, 16 * (NLOAD + 2))
            for l in range(LAYERS):
                v.wait_ge(wa_done, l + 1)
                nc.vector.tensor_copy(wx[:, l, TCOL:TCOL + 1], wh_ps[0:F, 1:2])
                nc.vector.tensor_copy(wx[:, l, SCOL:SCOL + 1], wh_ps[0:F, 0:1]).then_inc(wx_copied, 1)
            for g in range(GROUPS):
                copy_wh(g, g)

            def make_mask(k):
                v.wait_ge(adj_loaded[k % 3], 16 * (k // 3 + 1))
                if k >= 2:
                    v.wait_ge(codes_made, k - 1)
                nc.vector.tensor_scalar(masks[:, k % 2, :], arena[:, k % 3, :], 0, None, ALU.is_gt).then_inc(mask_made, 1)

            def top_rounds(dst, buf, width, room):
                cur = 0
                for r in range(room // 8):
                    link(nc.vector.max(out=dst[:, 8 * r:8 * r + 8], in_=buf[:, cur, 0:width]))
                    if r < room // 8 - 1:
                        link(nc.vector.match_replace(out=buf[:, 1 - cur, 0:width], in_to_replace=dst[:, 8 * r:8 * r + 8],
                                                     in_values=buf[:, cur, 0:width], imm_value=0.0))
                        cur = 1 - cur

            def list_edges(k):
                room, m = ROOM[k], CHUNKS[k]
                w = m * P
                v.wait_ge(codes_made, k + 1)
                both = codes_ps[k % 2][:, 0:TILES * (WORDS_C + 1)].rearrange("p (c w) -> p c w", w=WORDS_C + 1)
                words = both[:, :, 0:WORDS_C]
                k3 = key[:, 0, :].rearrange("p (c w) -> p c w", w=WORDS_C)
                b3 = word_base[:, :].rearrange("p (c w) -> p c w", w=WORDS_C)
                link(nc.vector.scalar_tensor_tensor(out=k3, in0=words, scalar=0.0, in1=b3, op0=ALU.is_gt, op1=ALU.mult))
                link(nc.vector.tensor_tensor(k3, k3, words, ALU.add))
                nc.vector.tensor_reduce(deg[:, k:k + 1], both[:, :, WORDS_C], AX, ALU.add).then_inc(codes_read, 1)
                v.wait_ge(codes_read, k + 1)
                nc.vector.tensor_copy(degb[:, :], deg[:, k:k + 1]).then_inc(deg_made, 1)
                top_rounds(top, key, WORDS, room)
                link(nc.vector.tensor_copy(topi[:, 0:room], top[:, 0:room]))
                link(nc.vector.tensor_scalar(word16[:, 0:room], topi[:, 0:room], BITS, 4,
                                             ALU.logical_shift_right, ALU.logical_shift_left))
                wide = [P, room, BITS]
                bv = bitv[:, 0:room * BITS].rearrange("p (r b) -> p r b", b=BITS)
                cv = colv[:, 0:room * BITS].rearrange("p (r b) -> p r b", b=BITS)
                link(nc.vector.tensor_tensor(bv, topi[:, 0:room].unsqueeze(2).broadcast_to(wide),
                                             bit_mask[:, :].unsqueeze(1).broadcast_to(wide), ALU.bitwise_and))
                link(nc.vector.tensor_tensor(cv, word16[:, 0:room].unsqueeze(2).broadcast_to(wide),
                                             bit_next[:, :].unsqueeze(1).broadcast_to(wide), ALU.add))
                link(nc.vector.scalar_tensor_tensor(out=cand[:, 0, 0:room * BITS], in0=bitv[:, 0:room * BITS], scalar=0.0,
                                                    in1=colv[:, 0:room * BITS], op0=ALU.is_gt, op1=ALU.mult))
                top_rounds(nbr, cand, room * BITS, room)
                link(nc.vector.tensor_scalar(nbrh[:, 0:room], nbr[:, 0:room], float(-1 - CENTER), None, ALU.add))
                v.wait_ge(off_made, k + 1)
                link(nc.vector.tensor_copy(nbrh[:, room:room + 1], off_ps[:, 0:1]))
                link(nc.vector.tensor_tensor(ends[:, k:k + 1], deg[:, k:k + 1], off_ps[:, 0:1], ALU.add))
                link(nc.vector.tensor_scalar(begun[:, 0:w], slot_row[:, 0:w], off_ps[:, 0:1], None, ALU.is_ge))
                nc.vector.scalar_tensor_tensor(out=inrow[:, 0:w], in0=slot_row[:, 0:w], scalar=ends[:, k:k + 1],
                                               in1=begun[:, 0:w], op0=ALU.is_lt, op1=ALU.mult).then_inc(slots_made, 1)
                v.wait_ge(slots_made, k + 1)
                link(nc.vector.tensor_scalar(penalty[:, BASE[k] * P:BASE[k + 1] * P], inrow[:, 0:w], 1.0, -MASKED,
                                             ALU.subtract, ALU.mult))
                for b, (c0, nb) in enumerate(slot_batches(k)):
                    v.wait_ge(list_made, BATCH0[k] + b + 1)
                    lists = list_ps[:, 0:nb * (room + 1)].rearrange("p (c r) -> p c r", r=room + 1)
                    shape = [P, nb, room]
                    pk = pick[:, 0:nb * room].rearrange("p (c r) -> p c r", r=room)
                    link(nc.vector.tensor_tensor(rank[:, 0:nb], slot_col[:, c0:c0 + nb], lists[:, :, room], ALU.subtract))
                    link(nc.vector.tensor_tensor(pk, room_row[:, 0:room].unsqueeze(1).broadcast_to(shape),
                                                 rank[:, 0:nb].unsqueeze(2).broadcast_to(shape), ALU.is_equal))
                    nc.vector.tensor_tensor(pk, pk, lists[:, :, 0:room], ALU.mult).then_inc(list_read, 1)
                    v.wait_ge(list_read, BATCH0[k] + b + 1)
                    link(nc.vector.tensor_reduce(picked[:, 0:nb], pk, AX, ALU.add))
                    link(nc.vector.tensor_scalar(index[:, BASE[k] + c0:BASE[k] + c0 + nb], picked[:, 0:nb], float(CENTER),
                                                 None, ALU.add))

            link(nc.vector.tensor_copy(before[:, :], before_f[:, :]))
            link(nc.vector.tensor_copy(packer[:, :], packer_f[:, :]))
            make_mask(0)
            for k in range(TILES):
                if k + 1 < TILES:
                    make_mask(k + 1)
                list_edges(k)
            link(nc.vector.tensor_scalar(lonely[:, :], deg[:, :], 0.0, None, ALU.is_equal))
            link(nc.vector.tensor_tensor(over[:, 0, :], deg[:, :], limits[:, 0, :], ALU.is_gt))
            link(nc.vector.tensor_tensor(over[:, 1, :], ends[:, :], limits[:, 1, :], ALU.is_gt))
            nc.vector.tensor_reduce(over_sum[:, :], over[:, :, :].rearrange("p a b -> p (a b)"), AX,
                                    ALU.add).then_inc(over_made, 1)
            v.wait_ge(over_summed, 1)
            nc.vector.tensor_scalar(flag[0:1, 0:1], off_ps[0:1, 0:1], 0.0, None, ALU.is_gt).then_inc(flag_made, 1)
            v.wait_ge(flag_made, 1)

            over_flag = v.value_load(flag[0:1, 0:1], min_val=0, max_val=1)

            def norm(link, y, xs, n, asked, answered, count, last):
                wide = [P, n, F]
                link(nc.vector.tensor_reduce(stat[:, 0:n], y, AX, ALU.add))
                link(nc.vector.tensor_scalar(stat[:, 0:n], stat[:, 0:n], -1.0 / F, None, ALU.mult))
                link(nc.vector.tensor_tensor(y, y, stat[:, 0:n].unsqueeze(2).broadcast_to(wide), ALU.add))
                link(nc.vector.tensor_tensor(num[:, 0:n, :], y, y, ALU.mult))
                link(nc.vector.tensor_reduce(stat[:, 0:n], num[:, 0:n, :], AX, ALU.add))
                nc.vector.tensor_scalar(var[:, 0:n], stat[:, 0:n], 1.0 / F, EPS, ALU.mult, ALU.add).then_inc(asked, 1)
                v.wait_ge(answered, count)
                link(nc.vector.tensor_tensor(stat[:, 0:n], rstd[:, 0:n], rstd[:, 0:n], ALU.mult))
                link(nc.vector.tensor_tensor(stat[:, 0:n], stat[:, 0:n], var[:, 0:n], ALU.mult))
                link(nc.vector.tensor_scalar(stat[:, 0:n], stat[:, 0:n], -0.5, 1.5, ALU.mult, ALU.add))
                link(nc.vector.tensor_tensor(stat[:, 0:n], stat[:, 0:n], rstd[:, 0:n], ALU.mult))
                last(nc.vector.tensor_tensor(xs, y, stat[:, 0:n].unsqueeze(2).broadcast_to(wide), ALU.mult))

            with v.If(over_flag == 0):
                def slope(l, g):
                    k = g * GROUP
                    nc.vector.tensor_scalar(sloped_own[:, k:k + GROUP], wh[:, k:k + GROUP, SCOL], ALPHA[l], None,
                                            ALU.mult).then_inc(slope_made, 1)

                def mask_scores(l, q):
                    k, c0, m = SEGS[q]
                    n = l * NSEG + q
                    c = (BASE[k] + c0) * P
                    y = score[:, n % YRING, 0:m * P]
                    v.wait_ge(sloped, n + 1)
                    link(nc.vector.scalar_tensor_tensor(out=y, in0=score_ps[n % 2][:, 0:m * P],
                                                        scalar=wh[:, k, SCOL:SCOL + 1], in1=y,
                                                        op0=ALU.add, op1=ALU.max))
                    nc.vector.tensor_tensor_reduce(out=y, in0=y, in1=penalty[:, c:c + m * P], scale=1.0, scalar=MASKED,
                                                   op0=ALU.add, op1=ALU.max,
                                                   accum_out=seg_max[:, q:q + 1]).then_inc(masked, 1)

                def row_maxima(l, k):
                    q = SEG0[k]
                    v.wait_ge(masked, l * NSEG + q + SEGN[k])
                    rm = seg_max[:, q:q + 1]
                    if SEGN[k] > 1:
                        rm = row_max[:, k:k + 1]
                        link(nc.vector.tensor_reduce(rm, seg_max[:, q:q + SEGN[k]], AX, ALU.max))
                    nc.vector.tensor_scalar(neg_max[:, k:k + 1], rm, FLOOR, -1.0, ALU.max, ALU.mult).then_inc(max_made, 1)

                def epilogue(l, g, e):
                    k0 = g * GROUP
                    wide = [P, GROUP, F]
                    v.wait_ge(agg_made, l * GROUPS + g + 1)
                    v.wait_ge(exped, l * NSEG + SEG0[k0 + GROUP - 1] + SEGN[k0 + GROUP - 1])
                    for j in range(GROUP):
                        q, n = SEG0[k0 + j], SEGN[k0 + j]
                        if n > 1:
                            link(nc.vector.tensor_reduce(den[:, j:j + 1], seg_sum[:, q:q + n], AX, ALU.add))
                        elif max(SEGN[k0:k0 + GROUP]) > 1:
                            link(nc.vector.tensor_copy(den[:, j:j + 1], seg_sum[:, q:q + 1]))
                    src = den[:, :] if max(SEGN[k0:k0 + GROUP]) > 1 else seg_sum[:, SEG0[k0]:SEG0[k0] + GROUP]
                    lone = lonely[:, k0:k0 + GROUP]
                    link(nc.vector.scalar_tensor_tensor(out=den[:, :], in0=lone, scalar=float(N), in1=src,
                                                        op0=ALU.mult, op1=ALU.add))
                    link(nc.vector.reciprocal(den[:, :], den[:, :]))
                    link(nc.vector.tensor_tensor(num[:, :, :], sum_wh[:, :].unsqueeze(1).broadcast_to(wide),
                                                 lone.unsqueeze(2).broadcast_to(wide), ALU.mult))
                    nc.vector.tensor_tensor(num[:, :, :], num[:, :, :],
                                            agg_ps[(l * GROUPS + g) % 2][:, 0:GROUP * F].rearrange("p (j f) -> p j f", j=GROUP),
                                            ALU.add).then_inc(agg_read, 1)
                    v.wait_ge(agg_read, l * GROUPS + g + 1)
                    link(nc.vector.tensor_tensor(num[:, :, :], num[:, :, :],
                                                 den[:, :].unsqueeze(2).broadcast_to(wide), ALU.mult))
                    xs = x[:, k0:k0 + GROUP, :]
                    if l == BIAS_LAYER:
                        link(nc.vector.tensor_tensor(num[:, :, :], num[:, :, :],
                                                     bias_sb[:, :].unsqueeze(1).broadcast_to(wide), ALU.add))
                    if ELU[l]:
                        nc.vector.tensor_scalar(low[:, :, :], num[:, :, :], 0.0, None, ALU.min).then_inc(elu_in, 1)
                        link(nc.vector.scalar_tensor_tensor(out=res[:, :, :], in0=num[:, :, :], scalar=0.0, in1=xs,
                                                            op0=ALU.max, op1=ALU.add))
                        v.wait_ge(elow_made, e)
                        link(nc.vector.scalar_tensor_tensor(out=res[:, :, :], in0=elow[:, :, :], scalar=-1.0,
                                                            in1=res[:, :, :], op0=ALU.add, op1=ALU.add))
                    else:
                        link(nc.vector.tensor_tensor(res[:, :, :], num[:, :, :], xs, ALU.add))

                    def last(ins):
                        ins.then_inc(x_made, 1)
                        v.wait_ge(x_made, l * GROUPS + g + 1)
                    norm(link, res[:, :, :], xs, GROUP, var_made, rstd_made, l * GROUPS + g + 1, last)

                e = 0
                for l in range(LAYERS):
                    v.wait_ge(sum_made, l + 1)
                    nc.vector.tensor_copy(sum_wh[:, :], wh_ps[:, 0:F]).then_inc(sum_copied, 1)
                    v.wait_ge(sum_copied, l + 1)
                    for g in range(GROUPS if l == 0 else 0):
                        slope(l, g)
                    for k in range(TILES + LAG_WH + 1):
                        if k < TILES:
                            for i in range(SEGN[k]):
                                mask_scores(l, SEG0[k] + i)
                            row_maxima(l, k)
                        if group_ended(k - LAG_EPILOGUE):
                            if ELU[l]:
                                e += 1
                            epilogue(l, (k - LAG_EPILOGUE) // GROUP, e)
                        if l < LAYERS - 1 and group_ended(k - LAG_WH):
                            g = (k - LAG_WH) // GROUP
                            copy_wh((l + 1) * GROUPS + g, g)
                            v.wait_ge(wh_copied, (l + 1) * GROUPS + g + 1)
                            slope(l + 1, g)
            with v.Else():
                nc.vector.memset(stat[:, 0:1], 0.0).then_inc(d_x, 1)
                v.wait_ge(d_x, 1)
                for l in range(LAYERS):
                    if l > 0:
                        for g in range(GROUPS):
                            copy_wh(l * GROUPS + g, g)
                    v.wait_ge(wh_copied, (l + 1) * GROUPS)
                    nc.vector.tensor_scalar(sloped_own[:, :], wh[:, :, SCOL], ALPHA[l], None, ALU.mult).then_inc(d_slope, 1)
                    own = wh[:, :, SCOL]
                    trow = arena[:, 3, :].bitcast(F32)
                    adj_sb, pen, z = arena[:, 0, :], arena[:, 1, :].bitcast(F32), arena[:, 2, :].bitcast(F32)
                    per = 21
                    with v.Fori(0, TILES) as k:
                        n = [0]

                        def dlink(ins):
                            n[0] += 1
                            ins.then_inc(d_dve, 1)
                            v.wait_ge(d_dve, (l * TILES + k) * per + n[0])
                        v.wait_ge(d_adj, (l * TILES + k + 1) * 16)
                        dlink(nc.vector.tensor_scalar(pen, adj_sb, 0, MASKED, ALU.is_le, ALU.mult))
                        v.wait_ge(d_z, l * TILES + k + 1)
                        dlink(nc.vector.scalar_tensor_tensor(out=z, in0=trow, scalar=own[:, bass.ds(k, 1)], in1=z,
                                                             op0=ALU.add, op1=ALU.max))
                        dlink(nc.vector.tensor_tensor(pen, pen, z, ALU.add))
                        dlink(nc.vector.tensor_reduce(row_max[:, 0:1], pen, AX, ALU.max))
                        nc.vector.tensor_scalar(neg_max[:, 0:1], row_max[:, 0:1], -1.0, None, ALU.mult).then_inc(d_max, 1)
                        v.wait_ge(d_agg, l * TILES + k + 1)
                        dlink(nc.vector.reciprocal(den[:, 0:1], seg_sum[:, 0:1]))
                        dlink(nc.vector.tensor_scalar(num[:, 0, :], agg_ps[0][:, 0:F], den[:, 0:1], None, ALU.mult))
                        xs = x[:, bass.ds(k, 1), :]
                        if l == BIAS_LAYER:
                            dlink(nc.vector.tensor_tensor(num[:, 0, :], num[:, 0, :], bias_sb[:, :], ALU.add))
                        nc.vector.tensor_scalar(low[:, 0, :], num[:, 0, :], 0.0, None, ALU.min).then_inc(d_low, 1)
                        if ELU[l]:
                            dlink(nc.vector.scalar_tensor_tensor(out=res[:, 0:1, :], in0=num[:, 0:1, :], scalar=0.0, in1=xs,
                                                                 op0=ALU.max, op1=ALU.add))
                            v.wait_ge(d_elow, l * TILES + k + 1)
                            dlink(nc.vector.scalar_tensor_tensor(out=res[:, 0:1, :], in0=elow[:, 0:1, :], scalar=-1.0,
                                                                 in1=res[:, 0:1, :], op0=ALU.add, op1=ALU.add))
                        else:
                            dlink(nc.vector.tensor_tensor(res[:, 0:1, :], num[:, 0:1, :], xs, ALU.add))
                            v.wait_ge(d_elow, l * TILES + k + 1)

                        def last(ins):
                            ins.then_inc(d_x, 1)
                            v.wait_ge(d_x, l * TILES + k + 2)
                        norm(dlink, res[:, 0:1, :], xs, 1, d_var, d_rstd, l * TILES + k + 1, last)
                        while n[0] < per:
                            dlink(nc.vector.tensor_copy(stat[:, 0:1], den[:, 0:1]))


def _constants():
    p = np.arange(P)
    packer = np.zeros((P, WORDS_C + 1), np.float32)
    packer[p, p // BITS] = 2.0 ** (p % BITS)
    packer[:, WORDS_C] = 1.0

    def rows(a):
        return np.ascontiguousarray(np.broadcast_to(a, (P, len(a))))
    return {
        "ident": np.eye(P, dtype=np.float32),
        "ones": np.ones((P, P), np.float32),
        "before": (p[:, None] < p[None, :]).astype(np.float32),
        "packer": packer,
        "word_base": rows(np.arange(WORDS, dtype=np.float32) * 2.0 ** BITS),
        "slot_row": rows(np.arange(MAXC * P, dtype=np.float32)),
        "slot_col": np.ascontiguousarray((np.arange(MAXC)[None, :] * P + p[:, None]).astype(np.float32)),
        "room_row": rows(np.arange(MAXR, dtype=np.float32)),
        "bit_mask": rows((1 << np.arange(BITS)).astype(np.int32)),
        "bit_next": rows(np.arange(1, BITS + 1, dtype=np.float32)),
        "limits": rows(np.array(ROOM + [P * c for c in CHUNKS], np.float32)),
    }


def kernel(x, adj, L0_gnn_W, L0_gnn_a, L1_gnn_weight_w, L1_gnn_weight_a, L1_gnn_bias,
           L2_gnn_W, L2_gnn_a, L3_gnn_W, L3_gnn_a):
    import numpy as _np
    import concourse.bacc as _bacc
    from concourse import mybir as _mybir
    from concourse.bass_utils import run_bass_kernel_spmd as _run

    adj = _np.asarray(adj)
    adj_t = adj.reshape(TILES, P, TILES, P).transpose(0, 3, 2, 1).reshape(TILES, P, N)
    feeds = {"x": x, "adj": adj, "adj_t": adj_t, "bias": L1_gnn_bias,
             "w0": L0_gnn_W, "w1": L1_gnn_weight_w, "w2": L2_gnn_W, "w3": L3_gnn_W,
             "a0": L0_gnn_a, "a1": L1_gnn_weight_a, "a2": L2_gnn_a, "a3": L3_gnn_a}
    for i in range(LAYERS):
        feeds[f"a{i}"] = _np.asarray(feeds[f"a{i}"]).reshape(2, F).T
    feeds.update({f"c_{n}": a for n, a in _constants().items()})

    nc = _bacc.Bacc("TRN2", target_bir_lowering=False, num_devices=1)
    arrays, aps = {}, {}
    for name, a in feeds.items():
        a = _np.ascontiguousarray(a)
        arrays[f"in_{name}"] = a
        aps[name] = nc.dram_tensor(f"in_{name}", a.shape, _mybir.dt.from_np(a.dtype), kind="ExternalInput").ap()
    out = nc.dram_tensor("out_x", (N, F), _mybir.dt.float32, kind="ExternalOutput").ap()
    gat_kernel(nc, aps["x"], aps["adj"], aps["adj_t"], [aps[f"w{i}"] for i in range(4)],
               [aps[f"a{i}"] for i in range(4)], aps["bias"],
               {n[2:]: a for n, a in aps.items() if n.startswith("c_")}, out)
    return _run(nc, [arrays], core_ids=[0]).results[0]["out_x"]
```

```python
from contextlib import ExitStack

import numpy as np

import concourse.bass as bass
from concourse import mybir

ALU = mybir.AluOpType
ACT = mybir.ActivationFunctionType
AX = mybir.AxisListType.X
F32 = mybir.dt.float32
F16 = mybir.dt.float16
BF16 = mybir.dt.bfloat16
I32 = mybir.dt.int32

P = 128
N = 4096
F = 64
TILES = N // P
LAYERS = 4
ALPHA = [0.2, 0.01, 0.2, 0.01]
ELU = [True, False, True, True]
BIAS_LAYER = 1
EPS = 1e-5
MASKED = -1e30
FLOOR = -1e20

BITS = 16
WORDS = N // BITS
WORDS_C = P // BITS
TCOL = F
SCOL = F + 1
WX = F + 2

CHUNKS = [13, 6, 5, 4, 4] + [3] * 8 + [2] * 19
ROOM = [96] + [24] * 3 + [16] * 16 + [8] * 12
BASE = [sum(CHUNKS[:k]) for k in range(TILES + 1)]
NCH = BASE[TILES]
MAXC = max(CHUNKS)
MAXR = max(ROOM)
CENTER = N // 2

BATCHES = [(0, 1), (1, 3)] + [(k, 4) for k in range(4, TILES, 4)]
BMAX = 4
for _k, _n in BATCHES:
    assert len(set(ROOM[_k:_k + _n])) == 1
MAXB = max(n * ROOM[k] for k, n in BATCHES)
MAXBC = max(sum(CHUNKS[k:k + n]) for k, n in BATCHES)
SPLIT = 2560

GROUP = 4
GROUPS = TILES // GROUP
SEG = 4
SEGS = []
for _k in range(TILES):
    for _c in range(0, CHUNKS[_k], SEG):
        SEGS.append((_k, _c, min(SEG, CHUNKS[_k] - _c)))
NSEG = len(SEGS)
SEG0 = [min(q for q in range(NSEG) if SEGS[q][0] == k) for k in range(TILES)]
SEGN = [sum(1 for s in SEGS if s[0] == k) for k in range(TILES)]
GROUP_END = [SEG0[g * GROUP + GROUP - 1] + SEGN[g * GROUP + GROUP - 1] for g in range(GROUPS)]
RING = 12
TRING = 8

LAG = {"spread": 0, "slope": 1, "mask": 1, "exp": 2, "turn": 3, "copy_turned": 4, "aggregate": 5,
       "combine": 6, "elu": 7, "center": 8, "rstd": 9, "scale": 11, "turn_x": 12, "copy_x": 13,
       "project": 14, "copy_wh": 15}
ROUNDS = TILES + max(LAG.values())


def tile_of(stage, i):
    k = i - LAG[stage]
    return k if 0 <= k < TILES else None


def segs(k):
    return () if k is None else range(SEG0[k], SEG0[k] + SEGN[k])


def group_of(stage, i):
    k = i - LAG[stage]
    return k // GROUP if 0 <= k < TILES and k % GROUP == GROUP - 1 else None


def slot_batches(k):
    per = 512 // (ROOM[k] + 1)
    return [(c, min(per, CHUNKS[k] - c)) for c in range(0, CHUNKS[k], per)]


BATCH0 = [sum(len(slot_batches(j)) for j in range(k)) for k in range(TILES + 1)]


def gat_kernel(nc, x_in, adj, adj_t, weights, avecs, bias, consts, out):
    with ExitStack() as ctx:
        def sb(name, shape, dt):
            return ctx.enter_context(nc.sbuf_tensor(name, shape, dt))

        def bank(name):
            return ctx.enter_context(nc.psum_tensor(name, [P, 512], F32))

        def sem(name):
            return ctx.enter_context(nc.semaphore(name))

        table = [nc.dram_tensor(f"table{l}", [N, WX], F32, kind="Internal").ap() for l in range(LAYERS)]

        ident = sb("ident", [P, P], F32)
        ones = sb("ones", [P, P], F32)
        before = sb("before", [P, P], BF16)
        packer = sb("packer", [P, WORDS_C + 1], BF16)
        before_f = sb("before_f", [P, P], F32)
        packer_f = sb("packer_f", [P, WORDS_C + 1], F32)
        word_base = sb("word_base", [P, WORDS], F32)
        slot_row = sb("slot_row", [P, MAXC * P], F32)
        slot_col = sb("slot_col", [P, MAXC], F32)
        room_row = sb("room_row", [P, MAXR], F32)
        bit_mask = sb("bit_mask", [P, BITS], I32)
        bit_next = sb("bit_next", [P, BITS], F32)
        wx = sb("wx", [F, LAYERS, WX], F32)
        wt = sb("wt", [F, F], F32)
        av = sb("av", [F, LAYERS, 2], F32)
        bias_sb = sb("bias_sb", [P, F], F32)

        x = sb("x", [P, TILES, F], F32)
        wh = sb("wh", [P, TILES, WX], F32)
        xt = sb("xt", [F, 2, GROUP * P], F32)
        sum_wh = sb("sum_wh", [P, F], F32)

        arena = sb("arena", [P, 4, N], I32)
        masks = arena[:, 3, :].bitcast(BF16).rearrange("p (b n) -> p b n", b=2)
        positive = sb("positive", [P, N - SPLIT], BF16)
        key = sb("key", [P, 2, BMAX, WORDS], F32)
        top = sb("top", [P, MAXB], F32)
        topi = sb("topi", [P, MAXB], I32)
        word16 = sb("word16", [P, MAXB], I32)
        word16_f = sb("word16_f", [P, MAXB], F32)
        bitv = sb("bitv", [P, MAXB * BITS], I32)
        colv = sb("colv", [P, MAXB * BITS], F32)
        cand = sb("cand", [P, 2, MAXB * BITS], F32)
        nbr = sb("nbr", [P, MAXB], F32)
        nbrh = sb("nbrh", [P, 2, MAXB + BMAX], F16)
        deg = sb("deg", [P, TILES], F32)
        degb = sb("degb", [P, BMAX], BF16)
        from_start = sb("from_start", [P, TILES], F32)
        from_end = sb("from_end", [P, TILES], F32)
        begun = sb("begun", [P, MAXBC * P], BF16)
        ended = sb("ended", [P, MAXBC * P], BF16)
        inrow = sb("inrow", [P, MAXBC * P], BF16)
        penalty = sb("penalty", [P, NCH * P], BF16)
        rank = sb("rank", [P, 2, MAXC], F32)
        pick = sb("pick", [P, 2, 512], F32)
        picked = sb("picked", [P, 2, MAXC], F32)
        index = sb("index", [P, NCH], I32)
        lonely = sb("lonely", [P, TILES], F32)
        over = sb("over", [P, 2, TILES], F32)
        over_sum = sb("over_sum", [P, 1], F32)
        limits = sb("limits", [P, 2, TILES], F32)
        flag = sb("flag", [1, 1], I32)

        xg = sb("xg", [P, NCH, WX], F32)
        score = arena[:, 0:2, :].bitcast(F32).rearrange("p a n -> p (a n)")[:, 0:RING * SEG * P].rearrange(
            "p (r n) -> p r n", r=RING)
        slots_t = arena[:, 2, :].bitcast(F32).rearrange("p (r n) -> p r n", r=TRING)
        dense_t = sb("dense_t", [P, SEG * P], F32)
        seg_max = sb("seg_max", [P, NSEG], F32)
        seg_sum = sb("seg_sum", [P, NSEG], F32)
        sloped_own = sb("sloped_own", [P, TILES], F32)
        row_max = sb("row_max", [P, TILES], F32)
        neg_max = sb("neg_max", [P, TILES], F32)
        den = sb("den", [P, GROUP], F32)
        num, res, low, elow = [key[:, i // 2, 2 * (i % 2):2 * (i % 2) + 2, :].rearrange(
            "p a (j f) -> p a j f", j=GROUP) for i in range(4)]
        stat = sb("stat", [P, 2, GROUP], F32)
        var = sb("var", [P, 2, GROUP], F32)
        rstd = sb("rstd", [P, 2, GROUP], F32)

        banks = [bank(f"bank{i}") for i in range(8)]
        codes_ps = banks[0:2]
        turned_ps = banks[0:2]
        score_ps = banks[2:4]
        off_ps = banks[2]
        list_ps = [banks[3], banks[4]]
        agg_ps = banks[4:6]
        xt_ps = banks[6]
        wh_ps = banks[7]

        loaded = sem("loaded")
        adj_loaded = [sem(f"adj_loaded{i}") for i in range(3)]
        wt_done = sem("wt_done")
        wt_copied = sem("wt_copied")
        wa_done = sem("wa_done")
        wx_copied = sem("wx_copied")
        dve = sem("dve")
        mask_made = sem("mask_made")
        codes_made = sem("codes_made")
        codes_read = sem("codes_read")
        deg_made = sem("deg_made")
        off_made = sem("off_made")
        slots_made = sem("slots_made")
        list_made = sem("list_made")
        list_read = sem("list_read")
        act = sem("act_steps")
        half_made = sem("half_made")
        keyed = sem("keyed")
        word_made = sem("word_made")
        word_turned = sem("word_turned")
        col_made = sem("col_made")
        col_used = sem("col_used")
        starts_made = sem("starts_made")
        ends_made = sem("ends_made")
        signed = sem("signed")
        over_made = sem("over_made")
        over_summed = sem("over_summed")
        flag_made = sem("flag_made")

        x_made = sem("x_made")
        xt_made = sem("xt_made")
        xt_copied = sem("xt_copied")
        wh_made = sem("wh_made")
        wh_copied = sem("wh_copied")
        written = sem("written")
        gathered = [sem(f"gathered{k}") for k in range(TILES)]
        sum_made = sem("sum_made")
        sum_copied = sem("sum_copied")
        score_made = sem("score_made")
        slope_made = sem("slope_made")
        sloped = sem("sloped")
        masked = sem("masked")
        leaky_made = sem("leaky_made")
        max_made = sem("max_made")
        exped = sem("exped")
        turned = sem("turned")
        turned_copied = sem("turned_copied")
        aggregated = sem("aggregated")
        agg_read = sem("agg_read")
        den_made = sem("den_made")
        res_made = sem("res_made")
        low_made = sem("low_made")
        elow_made = sem("elow_made")
        elu_in = sem("elu_in")
        var_made = sem("var_made")
        ln_made = sem("ln_made")
        rstd_made = sem("rstd_made")
        stored = sem("stored")

        d_proj = sem("d_proj")
        d_trow = sem("d_trow")
        d_trow_copied = sem("d_trow_copied")
        d_adj = sem("d_adj")
        d_pen = sem("d_pen")
        d_slope = sem("d_slope")
        d_z = sem("d_z")
        d_max = sem("d_max")
        d_exp = sem("d_exp")
        d_turned = sem("d_turned")
        d_turned_copied = sem("d_turned_copied")
        d_agg = sem("d_agg")
        d_low = sem("d_low")
        d_elow = sem("d_elow")
        d_var = sem("d_var")
        d_ln = sem("d_ln")
        d_rstd = sem("d_rstd")
        d_x = sem("d_x")
        d_dve = sem("d_dve")

        NLOAD = 11 + 2 * LAYERS
        block = ctx.enter_context(nc.Block())

        x_v = x_in.rearrange("(k p) f -> p k f", p=P)
        out_v = out.rearrange("(k p) f -> p k f", p=P)
        tab_v = [t.rearrange("(k p) f -> p k f", p=P) for t in table]

        def tcol_wide(ap):
            return ap.broadcast_to([P, P])

        @block.sync
        def _(sp):
            for dst, src in [(ident, "ident"), (ones, "ones"), (before_f, "before"), (packer_f, "packer"),
                             (word_base, "word_base"), (slot_row, "slot_row"),
                             (slot_col, "slot_col"), (room_row, "room_row"), (bit_mask, "bit_mask"),
                             (bit_next, "bit_next"), (limits, "limits")]:
                d = dst[:, :] if len(dst.shape) == 2 else dst[:, :, :].rearrange("p a b -> p (a b)")
                sp.dma_start(d, consts[src]).then_inc(loaded, 16)
            for l in range(LAYERS):
                sp.dma_start(wx[:, l, 0:F], weights[l]).then_inc(loaded, 16)
                sp.dma_start(av[:, l, :], avecs[l]).then_inc(loaded, 16)
            sp.dma_start(bias_sb[:, :], bias.rearrange("(o f) -> o f", o=1).broadcast_to([P, F])).then_inc(loaded, 16)
            sp.dma_start(x[:, :, :], x_v).then_inc(loaded, 16)
            for k in range(TILES):
                if k >= 3:
                    sp.wait_ge(mask_made, k - 2)
                    sp.wait_ge(act, k - 2)
                sp.dma_start(arena[:, k % 3, :], adj_t[k]).then_inc(adj_loaded[k % 3], 16)
            for g in range(GROUPS):
                sp.wait_ge(wh_copied, g + 1)
                sp.dma_start(tab_v[0][:, g * GROUP:(g + 1) * GROUP, :],
                             wh[:, g * GROUP:(g + 1) * GROUP, :]).then_inc(written, 16)
            sp.wait_ge(flag_made, 1)
            over_flag = sp.value_load(flag[0:1, 0:1], min_val=0, max_val=1)
            with sp.If(over_flag == 0):
                for l in range(LAYERS):
                    for g in range(GROUPS):
                        if l < LAYERS - 1:
                            n = (l + 1) * GROUPS + g
                            sp.wait_ge(wh_copied, n + 1)
                            sp.dma_start(tab_v[l + 1][:, g * GROUP:(g + 1) * GROUP, :],
                                         wh[:, g * GROUP:(g + 1) * GROUP, :]).then_inc(written, 16)
                        else:
                            sp.wait_ge(x_made, l * GROUPS + g + 1)
                            sp.dma_start(out_v[:, g * GROUP:(g + 1) * GROUP, :],
                                         x[:, g * GROUP:(g + 1) * GROUP, :]).then_inc(stored, 16)
                sp.wait_ge(stored, 16 * GROUPS)
                sp.wait_ge(written, 16 * LAYERS * GROUPS)
            with sp.Else():
                for l in range(LAYERS):
                    with sp.Fori(0, TILES) as k:
                        sp.wait_ge(d_x, l * TILES + k + 1)
                        sp.dma_start(arena[:, 0, :], adj[bass.ts(k, P), :]).then_inc(d_adj, 16)
                sp.wait_ge(d_x, LAYERS * TILES + 1)
                sp.dma_start(out_v, x[:, :, :]).then_inc(stored, 16)
                sp.wait_ge(stored, 16)
                sp.wait_ge(written, 16 * GROUPS)

        @block.gpsimd
        def _(pool):
            for b, (k0, n) in enumerate(BATCHES):
                places = n * ROOM[k0]
                wide = [P, places, BITS]
                pool.wait_ge(word_made, b + 1)
                nc.gpsimd.tensor_copy(word16_f[:, 0:places], word16[:, 0:places]).then_inc(word_turned, 1)
                pool.wait_ge(word_turned, b + 1)
                if b >= 1:
                    pool.wait_ge(col_used, b)
                nc.gpsimd.tensor_tensor(colv[:, 0:places * BITS].rearrange("p (r b) -> p r b", b=BITS),
                                        word16_f[:, 0:places].unsqueeze(2).broadcast_to(wide),
                                        bit_next[:, :].unsqueeze(1).broadcast_to(wide), ALU.add).then_inc(col_made, 1)
            pool.wait_ge(flag_made, 1)
            over_flag = pool.value_load(flag[0:1, 0:1], min_val=0, max_val=1)
            with pool.If(over_flag == 0):
                for l in range(LAYERS):
                    pool.wait_ge(written, 16 * (l + 1) * GROUPS)
                    for k in range(TILES):
                        if l > 0 and k % GROUP == 0:
                            pool.wait_ge(aggregated, (l - 1) * NSEG + GROUP_END[k // GROUP])
                        for c in range(BASE[k], BASE[k + 1]):
                            pool.indirect_dma_start(
                                out=xg[:, c, :], out_offset=None, in_=table[l][:, :],
                                in_offset=bass.IndirectOffsetOnAxis(ap=index[:, c:c + 1], axis=0),
                            ).then_inc(gathered[k], 16)

        @block.tensor
        def _(pe):
            def turn_rows(n, g):
                if n >= 1:
                    pe.wait_ge(xt_copied, n)
                for j in range(GROUP):
                    t = nc.tensor.transpose(xt_ps[0:F, j * P:(j + 1) * P], x[:, g * GROUP + j, :], ident[:, :])
                t.then_inc(xt_made, 1)

            def project_rows(n, l):
                pe.wait_ge(xt_copied, n + 1)
                if n >= 1:
                    pe.wait_ge(wh_copied, n)
                for j in range(GROUP):
                    t = nc.tensor.matmul(wh_ps[:, j * WX:(j + 1) * WX], xt[:, n % 2, j * P:(j + 1) * P],
                                         wx[:, l, :], start=True, stop=True)
                t.then_inc(wh_made, 1)

            def sum_rows(l):
                pe.wait_ge(wh_copied, (l + 1) * GROUPS)
                for k in range(TILES):
                    t = nc.tensor.matmul(wh_ps[:, 0:F], ones[:, :], wh[:, k, 0:F],
                                         start=(k == 0), stop=(k == TILES - 1))
                t.then_inc(sum_made, 1)

            pe.wait_ge(loaded, 16 * (NLOAD + 2))
            for l in range(LAYERS):
                if l >= 1:
                    pe.wait_ge(wx_copied, l)
                nc.tensor.transpose(xt_ps[0:F, 0:F], wx[:, l, 0:F], ident[0:F, 0:F]).then_inc(wt_done, 1)
                pe.wait_ge(wt_copied, l + 1)
                nc.tensor.matmul(wh_ps[0:F, 0:2], wt[:, :], av[:, l, :], start=True, stop=True).then_inc(wa_done, 1)
            pe.wait_ge(wx_copied, LAYERS)
            for g in range(GROUPS):
                turn_rows(g, g)
                project_rows(g, 0)

            def pack(k):
                pe.wait_ge(mask_made, k + 1)
                pe.wait_ge(half_made, k + 1)
                if k >= 2:
                    pe.wait_ge(codes_read, k - 1)
                for c in range(TILES):
                    t = nc.tensor.matmul(codes_ps[k % 2][:, c * (WORDS_C + 1):(c + 1) * (WORDS_C + 1)],
                                         masks[:, k % 2, c * P:(c + 1) * P], packer[:, :], start=True, stop=True)
                t.then_inc(codes_made, 1)

            def first_slots(b):
                pe.wait_ge(deg_made, b + 1)
                nc.tensor.matmul(off_ps[:, 0:BATCHES[b][1]], before[:, :], degb[:, 0:BATCHES[b][1]],
                                 start=True, stop=True).then_inc(off_made, 1)

            def lists(b):
                k0, n = BATCHES[b]
                w = ROOM[k0] + 1
                for k in range(k0, k0 + n):
                    pe.wait_ge(slots_made, k + 1)
                    for j, (c0, nb) in enumerate(slot_batches(k)):
                        q = BATCH0[k] + j
                        if q >= 2:
                            pe.wait_ge(list_read, q - 1)
                        for c in range(nb):
                            at = (BASE[k] - BASE[k0] + c0 + c) * P
                            t = nc.tensor.matmul(list_ps[q % 2][:, c * w:(c + 1) * w], inrow[:, at:at + P],
                                                 nbrh[:, b % 2, (k - k0) * w:(k - k0 + 1) * w], start=True, stop=True)
                        t.then_inc(list_made, 1)

            for b in range(len(BATCHES) + 1):
                if b < len(BATCHES):
                    k0, n = BATCHES[b]
                    for k in range(k0, k0 + n):
                        pack(k)
                    first_slots(b)
                if b >= 1:
                    lists(b - 1)
            pe.wait_ge(over_made, 1)
            nc.tensor.matmul(off_ps[:, 0:1], ones[:, :], over_sum[:, :], start=True, stop=True).then_inc(over_summed, 1)

            pe.wait_ge(flag_made, 1)
            over_flag = pe.value_load(flag[0:1, 0:1], min_val=0, max_val=1)
            with pe.If(over_flag == 0):
                def spread(l, q):
                    k, c0, m = SEGS[q]
                    n = l * NSEG + q
                    pe.wait_ge(gathered[k], 16 * CHUNKS[k] * (l + 1))
                    if n >= 2:
                        pe.wait_ge(masked, n - 1)
                    for c in range(m):
                        t = nc.tensor.transpose(score_ps[n % 2][:, c * P:(c + 1) * P],
                                                tcol_wide(xg[:, BASE[k] + c0 + c, TCOL:TCOL + 1]), ident[:, :])
                    t.then_inc(score_made, 1)

                def turn(l, q):
                    k, c0, m = SEGS[q]
                    n = l * NSEG + q
                    pe.wait_ge(exped, n + 1)
                    if n >= 2:
                        pe.wait_ge(turned_copied, n - 1)
                    for c in range(m):
                        t = nc.tensor.transpose(turned_ps[n % 2][:, c * P:(c + 1) * P],
                                                score[:, n % RING, c * P:(c + 1) * P], ident[:, :])
                    t.then_inc(turned, 1)

                def aggregate(l, q):
                    k, c0, m = SEGS[q]
                    n = l * NSEG + q
                    ng = l * GROUPS + k // GROUP
                    if k % GROUP == 0 and c0 == 0 and ng >= 2:
                        pe.wait_ge(agg_read, ng - 1)
                    pe.wait_ge(turned_copied, n + 1)
                    for c in range(m):
                        t = nc.tensor.matmul(agg_ps[ng % 2][:, (k % GROUP) * F:(k % GROUP + 1) * F],
                                             slots_t[:, n % TRING, c * P:(c + 1) * P],
                                             xg[:, BASE[k] + c0 + c, 0:F],
                                             start=(c0 + c == 0), stop=(c0 + c == CHUNKS[k] - 1))
                    t.then_inc(aggregated, 1)

                for l in range(LAYERS):
                    for i in range(ROUNDS):
                        g = group_of("project", i)
                        if g is not None and l < LAYERS - 1:
                            project_rows((l + 1) * GROUPS + g, l + 1)
                        g = group_of("turn_x", i)
                        if g is not None and l < LAYERS - 1:
                            pe.wait_ge(x_made, l * GROUPS + g + 1)
                            if g == 0:
                                pe.wait_ge(sum_copied, l + 1)
                            turn_rows((l + 1) * GROUPS + g, g)
                        k = tile_of("aggregate", i)
                        for q in segs(k):
                            aggregate(l, q)
                        k = tile_of("turn", i)
                        for q in segs(k):
                            turn(l, q)
                        k = tile_of("spread", i)
                        for q in segs(k):
                            spread(l, q)
                        if i == 1:
                            sum_rows(l)
            with pe.Else():
                for l in range(LAYERS):
                    if l > 0:
                        pe.wait_ge(d_x, l * TILES + 1)
                        for g in range(GROUPS):
                            turn_rows(l * GROUPS + g, g)
                            project_rows(l * GROUPS + g, l)
                    pe.wait_ge(wh_copied, (l + 1) * GROUPS)
                    for k in range(TILES):
                        n = l * TILES + k
                        if n >= 2:
                            pe.wait_ge(d_trow_copied, n - 1)
                        nc.tensor.transpose(banks[2 + n % 2][:, 0:P], tcol_wide(wh[:, k, TCOL:TCOL + 1]),
                                            ident[:, :]).then_inc(d_trow, 1)
                    with pe.Fori(0, TILES) as k:
                        pe.wait_ge(d_exp, l * TILES + k + 1)
                        p_f = arena[:, 2, :].bitcast(F32)
                        for c4 in range(TILES // 4):
                            for c in range(4):
                                t = nc.tensor.transpose(turned_ps[0][:, c * P:(c + 1) * P],
                                                        p_f[:, (4 * c4 + c) * P:(4 * c4 + c + 1) * P], ident[:, :])
                            t.then_inc(d_turned, 1)
                            pe.wait_ge(d_turned_copied, (l * TILES + k) * (TILES // 4) + c4 + 1)
                            for c in range(4):
                                t = nc.tensor.matmul(agg_ps[0][:, 0:F], dense_t[:, c * P:(c + 1) * P],
                                                     wh[:, 4 * c4 + c, 0:F],
                                                     start=(c4 + c == 0), stop=(c4 == TILES // 4 - 1 and c == 3))
                            if c4 == TILES // 4 - 1:
                                t.then_inc(d_agg, 1)

        @block.scalar
        def _(sc):
            def copy_xt(n):
                sc.wait_ge(xt_made, n + 1)
                if n >= 2:
                    sc.wait_ge(wh_made, n - 1)
                nc.scalar.copy(xt[:, n % 2, :], xt_ps[0:F, :]).then_inc(xt_copied, 1)

            def estimate_rstd(h, n, asked, logged, answered, count):
                sc.wait_ge(asked, count)
                nc.scalar.activation(rstd[:, h, 0:n], var[:, h, 0:n], ACT.Ln).then_inc(logged, 1)
                sc.wait_ge(logged, count)
                nc.scalar.activation(rstd[:, h, 0:n], rstd[:, h, 0:n], ACT.Exp, scale=-0.5).then_inc(answered, 1)

            nc.scalar.preload_act_table_set("natural_log_exp_and_others")
            for l in range(LAYERS):
                sc.wait_ge(wt_done, l + 1)
                if l >= 1:
                    sc.wait_ge(wa_done, l)
                nc.scalar.copy(wt[:, :], xt_ps[0:F, 0:F]).then_inc(wt_copied, 1)
            for g in range(GROUPS):
                copy_xt(g)

            def mask_share(k):
                sc.wait_ge(adj_loaded[k % 3], 16 * (k // 3 + 1))
                if k >= 1:
                    sc.wait_ge(half_made, k)
                nc.scalar.activation(positive[:, :], arena[:, k % 3, SPLIT:N], ACT.Relu).then_inc(act, 1)
                sc.wait_ge(act, k + 1)
                if k >= 2:
                    sc.wait_ge(codes_made, k - 1)
                nc.scalar.activation(masks[:, k % 2, SPLIT:N], positive[:, :], ACT.Sign).then_inc(half_made, 1)

            def slot_signs(b):
                k0, n = BATCHES[b]
                sc.wait_ge(ends_made, b + 1)
                if b >= 1:
                    sc.wait_ge(slots_made, k0)
                for k in range(k0, k0 + n):
                    at = (BASE[k] - BASE[k0]) * P
                    w = CHUNKS[k] * P
                    nc.scalar.activation(begun[:, at:at + w], slot_row[:, 0:w], ACT.Sign, bias=from_start[:, k:k + 1])
                    nc.scalar.activation(ended[:, at:at + w], slot_row[:, 0:w], ACT.Sign,
                                         bias=from_end[:, k:k + 1]).then_inc(signed, 1)

            for b in range(len(BATCHES) + 1):
                if b < len(BATCHES):
                    k0, n = BATCHES[b]
                    for k in range(k0, k0 + n):
                        mask_share(k)
                if b >= 1:
                    slot_signs(b - 1)

            sc.wait_ge(flag_made, 1)
            over_flag = sc.value_load(flag[0:1, 0:1], min_val=0, max_val=1)
            with sc.If(over_flag == 0):
                def slope(l, q):
                    k, c0, m = SEGS[q]
                    n = l * NSEG + q
                    sc.wait_ge(score_made, n + 1)
                    if n >= RING:
                        sc.wait_ge(turned, n - RING + 1)
                    if k % GROUP == 0 and c0 == 0:
                        sc.wait_ge(slope_made, l * GROUPS + k // GROUP + 1)
                    nc.scalar.activation(score[:, n % RING, 0:m * P], score_ps[n % 2][:, 0:m * P], ACT.Identity,
                                         bias=sloped_own[:, k:k + 1], scale=ALPHA[l]).then_inc(sloped, 1)

                def exponentials(l, q):
                    k, c0, m = SEGS[q]
                    n = l * NSEG + q
                    sc.wait_ge(max_made, l * TILES + k + 1)
                    s = score[:, n % RING, 0:m * P]
                    nc.scalar.activation(s, s, ACT.Exp, bias=neg_max[:, k:k + 1],
                                         accum_out=seg_sum[:, q:q + 1]).then_inc(exped, 1)

                def copy_turned(l, q):
                    k, c0, m = SEGS[q]
                    n = l * NSEG + q
                    sc.wait_ge(turned, n + 1)
                    if n >= TRING:
                        sc.wait_ge(aggregated, n - TRING + 1)
                    nc.scalar.copy(slots_t[:, n % TRING, 0:m * P], turned_ps[n % 2][:, 0:m * P]).then_inc(turned_copied, 1)

                def elu_part(l, g):
                    elus[0] += 1
                    sc.wait_ge(elu_in, elus[0])
                    nc.scalar.activation(elow[:, g % 2, :, :], low[:, g % 2, :, :], ACT.Exp).then_inc(elow_made, 1)

                elus = [0]
                for l in range(LAYERS):
                    for i in range(ROUNDS):
                        for q in segs(tile_of("copy_turned", i)):
                            copy_turned(l, q)
                        for q in segs(tile_of("slope", i)):
                            slope(l, q)
                        for q in segs(tile_of("exp", i)):
                            exponentials(l, q)
                        g = group_of("elu", i)
                        if g is not None and ELU[l]:
                            elu_part(l, g)
                        g = group_of("rstd", i)
                        if g is not None:
                            estimate_rstd(g % 2, GROUP, var_made, ln_made, rstd_made, l * GROUPS + g + 1)
                        g = group_of("copy_x", i)
                        if g is not None and l < LAYERS - 1:
                            copy_xt((l + 1) * GROUPS + g)
            with sc.Else():
                e = 0
                for l in range(LAYERS):
                    if l > 0:
                        for g in range(GROUPS):
                            copy_xt(l * GROUPS + g)
                    for k in range(TILES):
                        n = l * TILES + k
                        sc.wait_ge(d_trow, n + 1)
                        nc.scalar.copy(arena[:, 3, k * P:(k + 1) * P].bitcast(F32),
                                       banks[2 + n % 2][:, 0:P]).then_inc(d_trow_copied, 1)
                    z = arena[:, 2, :].bitcast(F32)
                    sc.wait_ge(d_trow_copied, (l + 1) * TILES)
                    sc.wait_ge(d_slope, l + 1)
                    with sc.Fori(0, TILES) as k:
                        sc.wait_ge(d_x, l * TILES + k + 1)
                        nc.scalar.activation(z, arena[:, 3, :].bitcast(F32), ACT.Identity,
                                             bias=sloped_own[:, bass.ds(k, 1)], scale=ALPHA[l]).then_inc(d_z, 1)
                        sc.wait_ge(d_max, l * TILES + k + 1)
                        nc.scalar.activation(z, arena[:, 1, :].bitcast(F32), ACT.Exp, bias=neg_max[:, 0:1],
                                             accum_out=seg_sum[:, 0:1]).then_inc(d_exp, 1)
                        for c4 in range(TILES // 4):
                            sc.wait_ge(d_turned, (l * TILES + k) * (TILES // 4) + c4 + 1)
                            nc.scalar.copy(dense_t[:, :], turned_ps[0][:, :]).then_inc(d_turned_copied, 1)
                        sc.wait_ge(d_low, l * TILES + k + 1)
                        nc.scalar.activation(elow[:, 0, 0, :], low[:, 0, 0, :], ACT.Exp).then_inc(d_elow, 1)
                        estimate_rstd(0, 1, d_var, d_ln, d_rstd, l * TILES + k + 1)

        @block.vector
        def _(v):
            steps = [0]

            def link(ins):
                steps[0] += 1
                ins.then_inc(dve, 1)
                v.wait_ge(dve, steps[0])

            def copy_wh(n, g):
                v.wait_ge(wh_made, n + 1)
                nc.vector.tensor_copy(wh[:, g * GROUP:(g + 1) * GROUP, :],
                                      wh_ps[:, 0:GROUP * WX].rearrange("p (j f) -> p j f", j=GROUP)).then_inc(wh_copied, 1)

            v.wait_ge(loaded, 16 * (NLOAD + 2))
            for l in range(LAYERS):
                v.wait_ge(wa_done, l + 1)
                nc.vector.tensor_copy(wx[:, l, TCOL:TCOL + 1], wh_ps[0:F, 1:2])
                nc.vector.tensor_copy(wx[:, l, SCOL:SCOL + 1], wh_ps[0:F, 0:1]).then_inc(wx_copied, 1)
            for g in range(GROUPS):
                copy_wh(g, g)

            lane = [(dve, 0)] * BMAX
            counts = {}

            def ready(j=None):
                for at in set(lane if j is None else [lane[j]]):
                    if at[1] > 0:
                        v.wait_ge(*at)

            def done(ins, j=None, signal=None):
                signal = signal or dve
                if signal is dve:
                    steps[0] += 1
                    count = steps[0]
                else:
                    count = counts[signal] = counts.get(signal, 0) + 1
                ins.then_inc(signal, 1)
                for t in range(BMAX) if j is None else [j]:
                    lane[t] = (signal, count)

            def make_mask(k):
                v.wait_ge(adj_loaded[k % 3], 16 * (k // 3 + 1))
                if k >= 2:
                    v.wait_ge(codes_made, k - 1)
                nc.vector.tensor_scalar(masks[:, k % 2, 0:SPLIT], arena[:, k % 3, 0:SPLIT], 0, None,
                                        ALU.is_gt).then_inc(mask_made, 1)

            def make_keys(k, j):
                v.wait_ge(codes_made, k + 1)
                both = codes_ps[k % 2][:, 0:TILES * (WORDS_C + 1)].rearrange("p (c w) -> p c w", w=WORDS_C + 1)
                words = both[:, :, 0:WORDS_C]
                k3 = key[:, 0, j, :].rearrange("p (c w) -> p c w", w=WORDS_C)
                b3 = word_base[:, :].rearrange("p (c w) -> p c w", w=WORDS_C)
                done(nc.vector.scalar_tensor_tensor(out=k3, in0=words, scalar=0.0, in1=b3, op0=ALU.is_gt,
                                                    op1=ALU.mult), j)
                done(nc.vector.tensor_reduce(deg[:, k:k + 1], both[:, :, WORDS_C], AX, ALU.add), j)
                ready(j)
                done(nc.vector.tensor_tensor(k3, k3, words, ALU.add), j, codes_read)

            def top_rounds(n, room, dst, buf, width):
                cur = 0
                for r in range(room // 8):
                    for j in range(n):
                        at = j * room + 8 * r
                        ready(j)
                        done(nc.vector.max(out=dst[:, at:at + 8], in_=buf(cur, j)), j)
                    if r < room // 8 - 1:
                        for j in range(n):
                            at = j * room + 8 * r
                            ready(j)
                            done(nc.vector.match_replace(out=buf(1 - cur, j), in_to_replace=dst[:, at:at + 8],
                                                         in_values=buf(cur, j), imm_value=0.0), j)
                        cur = 1 - cur

            def list_neighbours(b):
                k0, n = BATCHES[b]
                room = ROOM[k0]
                places = n * room
                ready()
                done(nc.vector.tensor_copy(degb[:, 0:n], deg[:, k0:k0 + n]), None, deg_made)
                top_rounds(n, room, top, lambda cur, j: key[:, cur, j, :], WORDS)
                ready()
                done(nc.vector.tensor_copy(topi[:, 0:places], top[:, 0:places]))
                ready()
                done(nc.vector.tensor_scalar(word16[:, 0:places], topi[:, 0:places], BITS, 4,
                                             ALU.logical_shift_right, ALU.logical_shift_left), None, word_made)
                wide = [P, places, BITS]
                done(nc.vector.tensor_tensor(bitv[:, 0:places * BITS].rearrange("p (r b) -> p r b", b=BITS),
                                             topi[:, 0:places].unsqueeze(2).broadcast_to(wide),
                                             bit_mask[:, :].unsqueeze(1).broadcast_to(wide), ALU.bitwise_and))
                v.wait_ge(off_made, b + 1)
                start, end = from_start[:, k0:k0 + n], from_end[:, k0:k0 + n]
                nc.vector.tensor_scalar(start, off_ps[:, 0:n], -1.0, 0.5, ALU.mult, ALU.add).then_inc(starts_made, 1)
                v.wait_ge(starts_made, b + 1)
                nc.vector.tensor_tensor(end, start, deg[:, k0:k0 + n], ALU.subtract).then_inc(ends_made, 1)
                lists_h = nbrh[:, b % 2, 0:n * (room + 1)].rearrange("p (t r) -> p t r", r=room + 1)
                nc.vector.tensor_copy(lists_h[:, :, room], off_ps[:, 0:n])
                ready()
                v.wait_ge(col_made, b + 1)
                done(nc.vector.scalar_tensor_tensor(out=cand[:, 0, 0:places * BITS], in0=bitv[:, 0:places * BITS],
                                                    scalar=0.0, in1=colv[:, 0:places * BITS], op0=ALU.is_gt,
                                                    op1=ALU.mult), None, col_used)
                w = room * BITS
                top_rounds(n, room, nbr, lambda cur, j: cand[:, cur, j * w:(j + 1) * w], w)
                ready()
                done(nc.vector.tensor_scalar(lists_h[:, :, 0:room], nbr[:, 0:places].rearrange("p (t r) -> p t r", r=room),
                                             float(-1 - CENTER), None, ALU.add))

            def mark_slots(b):
                k0, n = BATCHES[b]
                ready()
                for k in range(k0, k0 + n):
                    at, w = (BASE[k] - BASE[k0]) * P, CHUNKS[k] * P
                    v.wait_ge(signed, k + 1)
                    nc.vector.tensor_tensor(inrow[:, at:at + w], begun[:, at:at + w], ended[:, at:at + w],
                                            ALU.is_gt).then_inc(slots_made, 1)
                v.wait_ge(slots_made, k0 + n)
                done(nc.vector.tensor_scalar(penalty[:, BASE[k0] * P:BASE[k0 + n] * P],
                                             inrow[:, 0:(BASE[k0 + n] - BASE[k0]) * P], 1.0, -MASKED,
                                             ALU.subtract, ALU.mult))

            def pick_neighbours(b):
                k0, n = BATCHES[b]
                room = ROOM[k0]
                for k in range(k0, k0 + n):
                    for i, (c0, nb) in enumerate(slot_batches(k)):
                        q = BATCH0[k] + i
                        h = q % 2
                        v.wait_ge(list_made, q + 1)
                        lists = list_ps[h][:, 0:nb * (room + 1)].rearrange("p (c r) -> p c r", r=room + 1)
                        shape = [P, nb, room]
                        pk = pick[:, h, 0:nb * room].rearrange("p (c r) -> p c r", r=room)
                        rk = rank[:, h, 0:nb]
                        link(nc.vector.tensor_tensor(rk, slot_col[:, c0:c0 + nb], lists[:, :, room], ALU.subtract))
                        link(nc.vector.tensor_tensor(pk, room_row[:, 0:room].unsqueeze(1).broadcast_to(shape),
                                                     rk.unsqueeze(2).broadcast_to(shape), ALU.is_equal))
                        nc.vector.tensor_tensor(pk, pk, lists[:, :, 0:room], ALU.mult).then_inc(list_read, 1)
                        v.wait_ge(list_read, q + 1)
                        link(nc.vector.tensor_reduce(picked[:, h, 0:nb], pk, AX, ALU.add))
                        link(nc.vector.tensor_scalar(index[:, BASE[k] + c0:BASE[k] + c0 + nb], picked[:, h, 0:nb],
                                                     float(CENTER), None, ALU.add))

            link(nc.vector.tensor_copy(before[:, :], before_f[:, :]))
            link(nc.vector.tensor_copy(packer[:, :], packer_f[:, :]))
            make_mask(0)
            for b in range(len(BATCHES) + 1):
                if b < len(BATCHES):
                    k0, n = BATCHES[b]
                    for k in range(k0, k0 + n):
                        if k + 1 < TILES:
                            make_mask(k + 1)
                        make_keys(k, k - k0)
                if b >= 1:
                    mark_slots(b - 1)
                if b < len(BATCHES):
                    list_neighbours(b)
                if b >= 1:
                    pick_neighbours(b - 1)
            ready()
            link(nc.vector.tensor_scalar(lonely[:, :], deg[:, :], 0.0, None, ALU.is_equal))
            link(nc.vector.tensor_tensor(over[:, 0, :], deg[:, :], limits[:, 0, :], ALU.is_gt))
            link(nc.vector.tensor_tensor(over[:, 1, :], from_end[:, :], limits[:, 1, :], ALU.is_lt))
            nc.vector.tensor_reduce(over_sum[:, :], over[:, :, :].rearrange("p a b -> p (a b)"), AX,
                                    ALU.add).then_inc(over_made, 1)
            v.wait_ge(over_summed, 1)
            nc.vector.tensor_scalar(flag[0:1, 0:1], off_ps[0:1, 0:1], 0.0, None, ALU.is_gt).then_inc(flag_made, 1)
            v.wait_ge(flag_made, 1)

            over_flag = v.value_load(flag[0:1, 0:1], min_val=0, max_val=1)

            def center(link, h, n, asked):
                wide = [P, n, F]
                y, st, sq = res[:, h, 0:n, :], stat[:, h, 0:n], num[:, h, 0:n, :]
                link(nc.vector.tensor_reduce(st, y, AX, ALU.add))
                link(nc.vector.tensor_scalar(st, st, -1.0 / F, None, ALU.mult))
                link(nc.vector.tensor_tensor(y, y, st.unsqueeze(2).broadcast_to(wide), ALU.add))
                link(nc.vector.tensor_tensor(sq, y, y, ALU.mult))
                link(nc.vector.tensor_reduce(st, sq, AX, ALU.add))
                nc.vector.tensor_scalar(var[:, h, 0:n], st, 1.0 / F, EPS, ALU.mult, ALU.add).then_inc(asked, 1)

            def scale_rows(link, h, n, xs, answered, count, last):
                y, st, r, va = res[:, h, 0:n, :], stat[:, h, 0:n], rstd[:, h, 0:n], var[:, h, 0:n]
                v.wait_ge(answered, count)
                link(nc.vector.tensor_tensor(st, r, r, ALU.mult))
                link(nc.vector.tensor_tensor(st, st, va, ALU.mult))
                link(nc.vector.tensor_scalar(st, st, -0.5, 1.5, ALU.mult, ALU.add))
                link(nc.vector.tensor_tensor(st, st, r, ALU.mult))
                last(nc.vector.tensor_tensor(xs, y, st.unsqueeze(2).broadcast_to([P, n, F]), ALU.mult))

            with v.If(over_flag == 0):
                def slope(l, g):
                    k = g * GROUP
                    nc.vector.tensor_scalar(sloped_own[:, k:k + GROUP], wh[:, k:k + GROUP, SCOL], ALPHA[l], None,
                                            ALU.mult).then_inc(slope_made, 1)

                def mask_scores(l, k):
                    for q in segs(k):
                        _, c0, m = SEGS[q]
                        n = l * NSEG + q
                        y = score[:, n % RING, 0:m * P]
                        v.wait_ge(sloped, n + 1)
                        nc.vector.scalar_tensor_tensor(out=y, in0=score_ps[n % 2][:, 0:m * P],
                                                       scalar=wh[:, k, SCOL:SCOL + 1], in1=y,
                                                       op0=ALU.add, op1=ALU.max).then_inc(leaky_made, 1)
                        v.wait_ge(leaky_made, n + 1)
                        c = (BASE[k] + c0) * P
                        nc.vector.tensor_tensor_reduce(out=y, in0=y, in1=penalty[:, c:c + m * P], scale=1.0,
                                                       scalar=MASKED, op0=ALU.add, op1=ALU.max,
                                                       accum_out=seg_max[:, q:q + 1]).then_inc(masked, 1)
                    q = SEG0[k]
                    v.wait_ge(masked, l * NSEG + q + SEGN[k])
                    rm = seg_max[:, q:q + 1]
                    if SEGN[k] > 1:
                        rm = row_max[:, k:k + 1]
                        link(nc.vector.tensor_reduce(rm, seg_max[:, q:q + SEGN[k]], AX, ALU.max))
                    nc.vector.tensor_scalar(neg_max[:, k:k + 1], rm, FLOOR, -1.0, ALU.max, ALU.mult).then_inc(max_made, 1)

                def combine(l, g):
                    k0, h = g * GROUP, g % 2
                    wide = [P, GROUP, F]
                    y = num[:, h, :, :]
                    v.wait_ge(aggregated, l * NSEG + GROUP_END[g])
                    lone = lonely[:, k0:k0 + GROUP]
                    several = max(SEGN[k0:k0 + GROUP]) > 1
                    if several:
                        for j in range(GROUP):
                            q, n = SEG0[k0 + j], SEGN[k0 + j]
                            link(nc.vector.tensor_reduce(den[:, j:j + 1], seg_sum[:, q:q + n], AX, ALU.add))
                    src = den[:, :] if several else seg_sum[:, SEG0[k0]:SEG0[k0] + GROUP]
                    link(nc.vector.tensor_tensor(y, sum_wh[:, :].unsqueeze(1).broadcast_to(wide),
                                                 lone.unsqueeze(2).broadcast_to(wide), ALU.mult))
                    nc.vector.scalar_tensor_tensor(out=den[:, :], in0=lone, scalar=float(N), in1=src,
                                                   op0=ALU.mult, op1=ALU.add).then_inc(den_made, 1)
                    nc.vector.tensor_tensor(y, y, agg_ps[(l * GROUPS + g) % 2][:, 0:GROUP * F].rearrange(
                        "p (j f) -> p j f", j=GROUP), ALU.add).then_inc(agg_read, 1)
                    v.wait_ge(den_made, l * GROUPS + g + 1)
                    link(nc.vector.reciprocal(den[:, :], den[:, :]))
                    v.wait_ge(agg_read, l * GROUPS + g + 1)
                    link(nc.vector.tensor_tensor(y, y, den[:, :].unsqueeze(2).broadcast_to(wide), ALU.mult))
                    xs = x[:, k0:k0 + GROUP, :]
                    if l == BIAS_LAYER:
                        link(nc.vector.tensor_tensor(y, y, bias_sb[:, :].unsqueeze(1).broadcast_to(wide), ALU.add))
                    if ELU[l]:
                        nc.vector.tensor_scalar(low[:, h, :, :], y, 0.0, None, ALU.min).then_inc(elu_in, 1)
                        nc.vector.scalar_tensor_tensor(out=res[:, h, :, :], in0=y, scalar=0.0, in1=xs,
                                                       op0=ALU.max, op1=ALU.add).then_inc(res_made, 1)
                    else:
                        nc.vector.tensor_tensor(res[:, h, :, :], y, xs, ALU.add).then_inc(res_made, 1)

                elus = 0
                for l in range(LAYERS):
                    for i in range(ROUNDS):
                        if l == 0 and i == 0:
                            for g in range(GROUPS):
                                slope(0, g)
                        if i == 2:
                            v.wait_ge(sum_made, l + 1)
                            nc.vector.tensor_copy(sum_wh[:, :], wh_ps[:, 0:F]).then_inc(sum_copied, 1)
                            v.wait_ge(sum_copied, l + 1)
                        g = group_of("copy_wh", i)
                        if g is not None and l < LAYERS - 1:
                            copy_wh((l + 1) * GROUPS + g, g)
                            v.wait_ge(wh_copied, (l + 1) * GROUPS + g + 1)
                            slope(l + 1, g)
                        g = group_of("scale", i)
                        if g is not None:
                            def last(ins):
                                ins.then_inc(x_made, 1)
                            scale_rows(link, g % 2, GROUP, x[:, g * GROUP:(g + 1) * GROUP, :], rstd_made,
                                       l * GROUPS + g + 1, last)
                        g = group_of("center", i)
                        if g is not None:
                            v.wait_ge(res_made, l * GROUPS + g + 1)
                            if ELU[l]:
                                elus += 1
                                v.wait_ge(elow_made, elus)
                                y = res[:, g % 2, :, :]
                                link(nc.vector.scalar_tensor_tensor(out=y, in0=elow[:, g % 2, :, :], scalar=-1.0, in1=y,
                                                                    op0=ALU.add, op1=ALU.add))
                            center(link, g % 2, GROUP, var_made)
                        g = group_of("combine", i)
                        if g is not None:
                            combine(l, g)
                        k = tile_of("mask", i)
                        if k is not None:
                            mask_scores(l, k)
            with v.Else():
                nc.vector.memset(stat[:, 0, 0:1], 0.0).then_inc(d_x, 1)
                v.wait_ge(d_x, 1)
                for l in range(LAYERS):
                    if l > 0:
                        for g in range(GROUPS):
                            copy_wh(l * GROUPS + g, g)
                    v.wait_ge(wh_copied, (l + 1) * GROUPS)
                    nc.vector.tensor_scalar(sloped_own[:, :], wh[:, :, SCOL], ALPHA[l], None, ALU.mult).then_inc(d_slope, 1)
                    own = wh[:, :, SCOL]
                    trow = arena[:, 3, :].bitcast(F32)
                    adj_sb, pen, z = arena[:, 0, :], arena[:, 1, :].bitcast(F32), arena[:, 2, :].bitcast(F32)
                    per = 21
                    with v.Fori(0, TILES) as k:
                        n = [0]

                        def dlink(ins):
                            n[0] += 1
                            ins.then_inc(d_dve, 1)
                            v.wait_ge(d_dve, (l * TILES + k) * per + n[0])
                        v.wait_ge(d_adj, (l * TILES + k + 1) * 16)
                        dlink(nc.vector.tensor_scalar(pen, adj_sb, 0, MASKED, ALU.is_le, ALU.mult))
                        v.wait_ge(d_z, l * TILES + k + 1)
                        dlink(nc.vector.scalar_tensor_tensor(out=z, in0=trow, scalar=own[:, bass.ds(k, 1)], in1=z,
                                                             op0=ALU.add, op1=ALU.max))
                        dlink(nc.vector.tensor_tensor(pen, pen, z, ALU.add))
                        dlink(nc.vector.tensor_reduce(row_max[:, 0:1], pen, AX, ALU.max))
                        nc.vector.tensor_scalar(neg_max[:, 0:1], row_max[:, 0:1], -1.0, None, ALU.mult).then_inc(d_max, 1)
                        v.wait_ge(d_agg, l * TILES + k + 1)
                        dlink(nc.vector.reciprocal(den[:, 0:1], seg_sum[:, 0:1]))
                        dlink(nc.vector.tensor_scalar(num[:, 0, 0, :], agg_ps[0][:, 0:F], den[:, 0:1], None, ALU.mult))
                        xs = x[:, bass.ds(k, 1), :]
                        if l == BIAS_LAYER:
                            dlink(nc.vector.tensor_tensor(num[:, 0, 0, :], num[:, 0, 0, :], bias_sb[:, :], ALU.add))
                        nc.vector.tensor_scalar(low[:, 0, 0, :], num[:, 0, 0, :], 0.0, None, ALU.min).then_inc(d_low, 1)
                        if ELU[l]:
                            dlink(nc.vector.scalar_tensor_tensor(out=res[:, 0, 0:1, :], in0=num[:, 0, 0:1, :], scalar=0.0, in1=xs,
                                                                 op0=ALU.max, op1=ALU.add))
                            v.wait_ge(d_elow, l * TILES + k + 1)
                            dlink(nc.vector.scalar_tensor_tensor(out=res[:, 0, 0:1, :], in0=elow[:, 0, 0:1, :], scalar=-1.0,
                                                                 in1=res[:, 0, 0:1, :], op0=ALU.add, op1=ALU.add))
                        else:
                            dlink(nc.vector.tensor_tensor(res[:, 0, 0:1, :], num[:, 0, 0:1, :], xs, ALU.add))
                            v.wait_ge(d_elow, l * TILES + k + 1)

                        def last(ins):
                            ins.then_inc(d_x, 1)
                            v.wait_ge(d_x, l * TILES + k + 2)
                        center(dlink, 0, 1, d_var)
                        scale_rows(dlink, 0, 1, xs, d_rstd, l * TILES + k + 1, last)
                        while n[0] < per:
                            dlink(nc.vector.tensor_copy(stat[:, 0, 0:1], den[:, 0:1]))


def _constants():
    p = np.arange(P)
    packer = np.zeros((P, WORDS_C + 1), np.float32)
    packer[p, p // BITS] = 2.0 ** (p % BITS)
    packer[:, WORDS_C] = 1.0

    def rows(a):
        return np.ascontiguousarray(np.broadcast_to(a, (P, len(a))))
    return {
        "ident": np.eye(P, dtype=np.float32),
        "ones": np.ones((P, P), np.float32),
        "before": (p[:, None] < p[None, :]).astype(np.float32),
        "packer": packer,
        "word_base": rows(np.arange(WORDS, dtype=np.float32) * 2.0 ** BITS),
        "slot_row": rows(np.arange(MAXC * P, dtype=np.float32)),
        "slot_col": np.ascontiguousarray((np.arange(MAXC)[None, :] * P + p[:, None]).astype(np.float32)),
        "room_row": rows(np.arange(MAXR, dtype=np.float32)),
        "bit_mask": rows((1 << np.arange(BITS)).astype(np.int32)),
        "bit_next": rows(np.arange(1, BITS + 1, dtype=np.float32)),
        "limits": rows(np.array(ROOM + [-P * c for c in CHUNKS], np.float32)),
    }


def kernel(x, adj, L0_gnn_W, L0_gnn_a, L1_gnn_weight_w, L1_gnn_weight_a, L1_gnn_bias,
           L2_gnn_W, L2_gnn_a, L3_gnn_W, L3_gnn_a):
    import numpy as _np
    import concourse.bacc as _bacc
    from concourse import mybir as _mybir
    from concourse.bass_utils import run_bass_kernel_spmd as _run

    adj = _np.asarray(adj)
    adj_t = adj.reshape(TILES, P, TILES, P).transpose(0, 3, 2, 1).reshape(TILES, P, N)
    feeds = {"x": x, "adj": adj, "adj_t": adj_t, "bias": L1_gnn_bias,
             "w0": L0_gnn_W, "w1": L1_gnn_weight_w, "w2": L2_gnn_W, "w3": L3_gnn_W,
             "a0": L0_gnn_a, "a1": L1_gnn_weight_a, "a2": L2_gnn_a, "a3": L3_gnn_a}
    for i in range(LAYERS):
        feeds[f"a{i}"] = _np.asarray(feeds[f"a{i}"]).reshape(2, F).T
    feeds.update({f"c_{n}": a for n, a in _constants().items()})

    nc = _bacc.Bacc("TRN2", target_bir_lowering=False, num_devices=1)
    arrays, aps = {}, {}
    for name, a in feeds.items():
        a = _np.ascontiguousarray(a)
        arrays[f"in_{name}"] = a
        aps[name] = nc.dram_tensor(f"in_{name}", a.shape, _mybir.dt.from_np(a.dtype), kind="ExternalInput").ap()
    out = nc.dram_tensor("out_x", (N, F), _mybir.dt.float32, kind="ExternalOutput").ap()
    gat_kernel(nc, aps["x"], aps["adj"], aps["adj_t"], [aps[f"w{i}"] for i in range(4)],
               [aps[f"a{i}"] for i in range(4)], aps["bias"],
               {n[2:]: a for n, a in aps.items() if n.startswith("c_")}, out)
    return _run(nc, [arrays], core_ids=[0]).results[0]["out_x"]
```

```python
from contextlib import ExitStack

import numpy as np

import concourse.bass as bass
from concourse import mybir

ALU = mybir.AluOpType
ACT = mybir.ActivationFunctionType
AX = mybir.AxisListType.X
F32 = mybir.dt.float32
F16 = mybir.dt.float16
BF16 = mybir.dt.bfloat16
I32 = mybir.dt.int32

P = 128
N = 4096
F = 64
TILES = N // P
LAYERS = 4
ALPHA = [0.2, 0.01, 0.2, 0.01]
ELU = [True, False, True, True]
BIAS_LAYER = 1
EPS = 1e-5
MASKED = -1e30
FLOOR = -1e20

BITS = 16
WORDS = N // BITS
WORDS_C = P // BITS
TCOL = F
SCOL = F + 1
WX = F + 2

UNIT = 64
UNITS = [24, 11, 9, 8, 7, 7, 6, 6] + [5] * 4 + [4] * 12 + [3] * 8
ROOM = [96] + [16] * 19 + [8] * 12
_UBASE = [sum(UNITS[:k]) for k in range(TILES + 1)]
OFFSET = [_UBASE[k] * UNIT % P for k in range(TILES)]
FIRST = [_UBASE[k] * UNIT // P for k in range(TILES + 1)]
CHUNKS = [-(-(OFFSET[k] + UNITS[k] * UNIT) // P) for k in range(TILES)]
PLACE = [sum(CHUNKS[:k]) for k in range(TILES + 1)]
NCH = FIRST[TILES]
assert _UBASE[TILES] * UNIT % P == 0
MAXC = max(CHUNKS)
MAXR = max(ROOM)
TILES_OF_CHUNK = [[k for k in range(TILES) if FIRST[k] <= c < FIRST[k] + CHUNKS[k]] for c in range(NCH)]
OWN = [sum(1 for t in TILES_OF_CHUNK if t[0] == k) for k in range(TILES)]
CENTER = N // 2

BATCHES = [(0, 1), (1, 3)] + [(k, 4) for k in range(4, TILES - 4, 4)] + [(TILES - 4, 2), (TILES - 2, 2)]
BMAX = 4
PART = 16
PART_ROOM = 24
LANES = max(ROOM) // PART
SPLIT = 2
for _k, _n in BATCHES:
    assert len(set(ROOM[_k:_k + _n])) == 1 and OFFSET[_k] == 0
MAXB = max(n * ROOM[k] for k, n in BATCHES)
MAXBC = max(sum(CHUNKS[k:k + n]) for k, n in BATCHES)
CODE_BANKS = 3
GATHER_START = 3
GATHER_SHARE = 3

GROUP = 4
GROUPS = TILES // GROUP
SEG = 4
SEGS = []
for _k in range(TILES):
    for _c in range(0, CHUNKS[_k], SEG):
        SEGS.append((_k, _c, min(SEG, CHUNKS[_k] - _c)))
NSEG = len(SEGS)
SEG0 = [min(q for q in range(NSEG) if SEGS[q][0] == k) for k in range(TILES)]
SEGN = [sum(1 for s in SEGS if s[0] == k) for k in range(TILES)]
GROUP_END = [SEG0[g * GROUP + GROUP - 1] + SEGN[g * GROUP + GROUP - 1] for g in range(GROUPS)]
RING = 12
TRING = 8

LAG = {"spread": 0, "slope": 1, "mask": 2, "exp": 2, "turn": 3, "copy_turned": 4, "aggregate": 4,
       "combine": 5, "elu": 6, "center": 7, "rstd": 8, "scale": 10, "turn_x": 11, "copy_x": 12,
       "project": 14, "copy_wh": 15, "own": 15}
ROUNDS = TILES + max(LAG.values())


def tile_of(stage, i):
    k = i - LAG[stage]
    return k if 0 <= k < TILES else None


def segs(k):
    return () if k is None else range(SEG0[k], SEG0[k] + SEGN[k])


def group_of(stage, i):
    k = i - LAG[stage]
    return k // GROUP if 0 <= k < TILES and k % GROUP == GROUP - 1 else None


CONST_WIDTHS = [P, P, P, WORDS_C + 1, NCH, MAXR, BITS, TILES, 2 * TILES]


def pieces(b):
    k0, n = BATCHES[b]
    per = 512 // (ROOM[k0] + 1)
    total = FIRST[k0 + n] - FIRST[k0]
    return [(c, min(per, total - c)) for c in range(0, total, per)]


PIECE0 = [sum(len(pieces(j)) for j in range(b)) for b in range(len(BATCHES) + 1)]


def gat_kernel(nc, x_in, adj, adj_t, weights, bias, consts, out):
    with ExitStack() as ctx:
        def sb(name, shape, dt):
            return ctx.enter_context(nc.sbuf_tensor(name, shape, dt))

        def bank(name):
            return ctx.enter_context(nc.psum_tensor(name, [P, 512], F32))

        def sem(name):
            return ctx.enter_context(nc.semaphore(name))

        table = [nc.dram_tensor(f"table{l}", [N, WX], F32, kind="Internal").ap() for l in range(LAYERS)]

        packed = sb("packed", [P, sum(CONST_WIDTHS)], F32)
        ident, ones, before_f, packer_f, slot_col, room_row, bit_next, half_less, limits_row = [
            packed[:, sum(CONST_WIDTHS[:i]):sum(CONST_WIDTHS[:i + 1])] for i in range(len(CONST_WIDTHS))]
        limits = limits_row.rearrange("p (a k) -> p a k", a=2)
        before = sb("before", [P, P], BF16)
        packer = sb("packer", [P, WORDS_C + 1], BF16)
        half = sb("half", [P, 1], F32)
        ones_b = sb("ones_b", [P, P], BF16)
        found = sb("found", [P, 2, LANES * PART_ROOM], F32)
        fix_f = sb("fix_f", [3, TILES * (WORDS_C + 1)], F32)
        fix = sb("fix", [3, TILES * (WORDS_C + 1)], BF16)
        ident_b = sb("ident_b", [P, P], BF16)
        slot_row = sb("slot_row", [P, MAXC * P], F32)
        bit_mask = sb("bit_mask", [P, BITS], I32)
        wx = sb("wx", [F, LAYERS, WX], F32)
        wt = sb("wt", [F, F], F32)
        bias_sb = sb("bias_sb", [P, F], F32)

        x = sb("x", [P, TILES, F], F32)
        wh = sb("wh", [P, TILES, WX], F32)
        xt = sb("xt", [F, 2, GROUP * P], F32)
        xsum = sb("xsum", [F, GROUPS], F32)
        sum_wh = sb("sum_wh", [P, F], F32)

        arena = sb("arena", [P, 4, N], I32)
        masks = arena[:, 3, :].bitcast(BF16).rearrange("p (b n) -> p b n", b=2)
        key = sb("key", [P, 2, BMAX, WORDS], F32)
        top = sb("top", [P, MAXB], F32)
        topi = sb("topi", [P, MAXB], I32)
        word = sb("word", [P, MAXB], I32)
        word_f = sb("word_f", [P, MAXB], F32)
        bitv = sb("bitv", [P, MAXB * BITS], I32)
        colv = sb("colv", [P, MAXB * BITS], F32)
        cand = sb("cand", [P, 2, MAXB * BITS], F32)
        nbr = sb("nbr", [P, MAXB], F32)
        nbrh = sb("nbrh", [P, 2, MAXB + BMAX], F16)
        deg = sb("deg", [P, TILES], F32)
        degb = sb("degb", [P, BMAX], BF16)
        from_start = sb("from_start", [P, TILES], F32)
        from_end = sb("from_end", [P, TILES], F32)
        begun = sb("begun", [P, MAXBC * P], BF16)
        ended = sb("ended", [P, MAXBC * P], BF16)
        inrow = sb("inrow", [P, MAXBC * P], BF16)
        penalty = sb("penalty", [P, PLACE[TILES] * P], BF16)
        rank = sb("rank", [P, 2, MAXBC], F32)
        pick = sb("pick", [P, 2, 512], F32)
        picked = sb("picked", [P, 2, MAXBC], F32)
        index = sb("index", [P, NCH], I32)
        lonely = sb("lonely", [P, TILES], F32)
        over = sb("over", [P, 2, TILES], F32)
        over_sum = sb("over_sum", [P, 1], F32)
        flag = sb("flag", [1, 1], I32)

        xg = sb("xg", [P, NCH, WX], F32)
        score = arena[:, 0:2, :].bitcast(F32).rearrange("p a n -> p (a n)")[:, 0:RING * SEG * P].rearrange(
            "p (r n) -> p r n", r=RING)
        slots_t = arena[:, 2, :].bitcast(F32).rearrange("p (r n) -> p r n", r=TRING)
        dense_t = sb("dense_t", [P, SEG * P], F32)
        seg_max = sb("seg_max", [P, NSEG], F32)
        seg_sum = sb("seg_sum", [P, NSEG], F32)
        sloped_own = sb("sloped_own", [P, TILES], F32)
        row_max = sb("row_max", [P, TILES], F32)
        neg_max = sb("neg_max", [P, TILES], F32)
        den = sb("den", [P, GROUP], F32)
        num, res, low, elow = [key[:, i // 2, 2 * (i % 2):2 * (i % 2) + 2, :].rearrange(
            "p a (j f) -> p a j f", j=GROUP) for i in range(4)]
        lone_rows = arena[:, 3, 0:TILES * F].bitcast(F32).rearrange("p (k f) -> p k f", k=TILES)
        stats = sb("stats", [P, GROUP, 6], F32)
        mean_var = sb("mean_var", [P, 2, GROUP, 2], F32)
        stat = sb("stat", [P, 2, GROUP], F32)
        var = sb("var", [P, 2, GROUP], F32)
        rstd = sb("rstd", [P, 2, GROUP], F32)

        banks = [bank(f"bank{i}") for i in range(8)]
        codes_ps = [banks[0], banks[1], banks[5]]
        turned_ps = banks[0:2]
        score_ps = [banks[2], banks[3]]
        off_ps = banks[2]
        list_ps = [banks[3], banks[4]]
        agg_ps = banks[4:6]
        xt_ps, wh_ps = banks[7], banks[6]

        loaded = sem("loaded")
        x_loaded = sem("x_loaded")
        slots_loaded = sem("slots_loaded")
        centered = sem("centered")
        adj_loaded = [sem(f"adj_loaded{i}") for i in range(3)]
        wt_done = sem("wt_done")
        wt_copied = sem("wt_copied")
        wa_done = sem("wa_done")
        wx_copied = sem("wx_copied")
        dve = sem("dve")
        mask_made = sem("mask_made")
        codes_made = sem("codes_made")
        codes_read = sem("codes_read")
        nbr_made = sem("nbr_made")
        cast_made = sem("cast_made")
        deg_made = sem("deg_made")
        off_made = sem("off_made")
        slots_made = sem("slots_made")
        list_made = sem("list_made")
        list_read = sem("list_read")
        word_made = sem("word_made")
        word_turned = sem("word_turned")
        col_made = sem("col_made")
        col_used = sem("col_used")
        starts_made = sem("starts_made")
        ends_made = sem("ends_made")
        signed = sem("signed")
        penalty_made = sem("penalty_made")
        index_made = sem("index_made")
        over_made = sem("over_made")
        over_summed = sem("over_summed")
        flag_made = sem("flag_made")

        x_made = sem("x_made")
        xt_made = sem("xt_made")
        xt_copied = sem("xt_copied")
        wh_made = sem("wh_made")
        wh_copied = sem("wh_copied")
        written = sem("written")
        gathered = [sem(f"gathered{k}") for k in range(TILES)]
        sum_made = sem("sum_made")
        sum_copied = sem("sum_copied")
        score_made = sem("score_made")
        slope_made = sem("slope_made")
        sloped = sem("sloped")
        masked = sem("masked")
        max_made = sem("max_made")
        exped = sem("exped")
        turned = sem("turned")
        turned_copied = sem("turned_copied")
        aggregated = sem("aggregated")
        agg_read = sem("agg_read")
        res_made = sem("res_made")
        elow_made = sem("elow_made")
        var_made = sem("var_made")
        ln_made = sem("ln_made")
        rstd_made = sem("rstd_made")
        stored = sem("stored")

        d_trow = sem("d_trow")
        d_trow_copied = sem("d_trow_copied")
        d_adj = sem("d_adj")
        d_slope = sem("d_slope")
        d_z = sem("d_z")
        d_max = sem("d_max")
        d_exp = sem("d_exp")
        d_turned = sem("d_turned")
        d_turned_copied = sem("d_turned_copied")
        d_agg = sem("d_agg")
        d_low = sem("d_low")
        d_elow = sem("d_elow")
        d_var = sem("d_var")
        d_ln = sem("d_ln")
        d_rstd = sem("d_rstd")
        d_x = sem("d_x")
        d_dve = sem("d_dve")

        NLOAD = 4
        block = ctx.enter_context(nc.Block())

        tab_v = [t.rearrange("(p k) f -> p k f", p=P) for t in table]

        def tcol_wide(ap):
            return ap.broadcast_to([P, P])

        @block.sync
        def _(sp):
            sp.dma_start(wx[:, :, :], weights).then_inc(loaded, 16)
            sp.dma_start(packed[:, :], consts["packed"]).then_inc(loaded, 16)
            sp.dma_start(fix_f[:, :], consts["fix"]).then_inc(loaded, 16)
            sp.dma_start(bit_mask[:, :], consts["bit_mask"]).then_inc(loaded, 16)
            for k in range(TILES):
                if k >= 3:
                    sp.wait_ge(mask_made, k - 2)
                sp.dma_start(arena[:, k % 3, :], adj_t[k]).then_inc(adj_loaded[k % 3], 16)
                if k == 0:
                    sp.dma_start(x[:, :, :], x_in).then_inc(x_loaded, 16)
                    sp.dma_start(slot_row[:, :], consts["slot_row"]).then_inc(slots_loaded, 16)
                    sp.dma_start(bias_sb[:, :], bias.rearrange("(o f) -> o f", o=1).broadcast_to([P, F])).then_inc(
                        slots_loaded, 16)
            sp.wait_ge(flag_made, 1)
            over_flag = sp.value_load(flag[0:1, 0:1], min_val=0, max_val=1)
            with sp.If(over_flag == 0):
                for l in range(LAYERS):
                    for g in range(GROUPS):
                        if l < LAYERS - 1:
                            n = (l + 1) * GROUPS + g
                            sp.wait_ge(wh_copied, n + 1)
                            sp.dma_start(tab_v[l + 1][:, g * GROUP:(g + 1) * GROUP, :],
                                         wh[:, g * GROUP:(g + 1) * GROUP, :]).then_inc(written, 16)
                        else:
                            sp.wait_ge(x_made, l * GROUPS + g + 1)
                            sp.dma_start(out[:, g * GROUP:(g + 1) * GROUP, :],
                                         x[:, g * GROUP:(g + 1) * GROUP, :]).then_inc(stored, 16)
                sp.wait_ge(stored, 16 * GROUPS)
                sp.wait_ge(written, 16 * (1 + (LAYERS - 1) * GROUPS))
            with sp.Else():
                for l in range(LAYERS):
                    with sp.Fori(0, TILES) as k:
                        sp.wait_ge(d_x, l * TILES + k + 1)
                        sp.dma_start(arena[:, 0, :], adj[bass.ts(k, P), :]).then_inc(d_adj, 16)
                sp.wait_ge(d_x, LAYERS * TILES + 1)
                sp.dma_start(out, x[:, :, :]).then_inc(stored, 16)
                sp.wait_ge(stored, 16)
                sp.wait_ge(written, 16)

        @block.gpsimd
        def _(pool):
            def slot_rows(b):
                k0, n = BATCHES[b]
                if b >= 1:
                    pool.wait_ge(penalty_made, b)
                    pool.wait_ge(list_made, PIECE0[b])
                for k in range(k0, k0 + n):
                    at, w = (PLACE[k] - PLACE[k0]) * P, CHUNKS[k] * P
                    pool.wait_ge(signed, k + 1)
                    nc.gpsimd.tensor_tensor(inrow[:, at:at + w], begun[:, at:at + w], ended[:, at:at + w],
                                            ALU.subtract).then_inc(slots_made, 1)

            def columns(b):
                k0, n = BATCHES[b]
                places = n * ROOM[k0]
                wide = [P, places, BITS]
                pool.wait_ge(word_made, b + 1)
                nc.gpsimd.tensor_copy(word_f[:, 0:places], word[:, 0:places]).then_inc(word_turned, 1)
                pool.wait_ge(word_turned, b + 1)
                if b >= 1:
                    pool.wait_ge(col_used, b)
                nc.gpsimd.tensor_tensor(colv[:, 0:places * BITS].rearrange("p (r b) -> p r b", b=BITS),
                                        word_f[:, 0:places].unsqueeze(2).broadcast_to(wide),
                                        bit_next[:, :].unsqueeze(1).broadcast_to(wide), ALU.add).then_inc(col_made, 1)

            def gather(l, k, c):
                pool.indirect_dma_start(
                    out=xg[:, c, :], out_offset=None, in_=table[l][:, :],
                    in_offset=bass.IndirectOffsetOnAxis(ap=index[:, c:c + 1], axis=0),
                ).then_inc(gathered[k], 16)

            def gather_some(count, made):
                for c in range(started[0], min(started[0] + count, FIRST[BATCHES[made][0]] if made < len(BATCHES) else NCH)):
                    k = TILES_OF_CHUNK[c][0]
                    b = [b for b, (k0, n) in enumerate(BATCHES) if k0 <= k < k0 + n][0]
                    if started[0] == 0 or c == FIRST[BATCHES[b][0]]:
                        pool.wait_ge(index_made, b + 1)
                    gather(0, k, c)
                    started[0] += 1

            started = [0]
            pool.wait_ge(loaded, 16 * NLOAD)
            for b in range(len(BATCHES)):
                if b == GATHER_START:
                    pool.wait_ge(written, 16)
                if b >= 1:
                    slot_rows(b - 1)
                columns(b)
                if GATHER_START <= b < len(BATCHES) - 1:
                    gather_some(GATHER_SHARE * BATCHES[b][1], b - 1)
            slot_rows(len(BATCHES) - 1)
            gather_some(NCH, len(BATCHES) - 1)
            gather_some(NCH, len(BATCHES))
            pool.wait_ge(flag_made, 1)
            over_flag = pool.value_load(flag[0:1, 0:1], min_val=0, max_val=1)
            with pool.If(over_flag == 0):
                for l in range(1, LAYERS):
                    pool.wait_ge(written, 16 * (1 + l * GROUPS))
                    for k in range(TILES):
                        if k % GROUP == 0:
                            pool.wait_ge(aggregated, (l - 1) * NSEG + GROUP_END[k // GROUP])
                        for c in range(FIRST[k] + CHUNKS[k] - OWN[k], FIRST[k] + CHUNKS[k]):
                            gather(l, k, c)
            with pool.Else():
                for k in range(TILES):
                    pool.wait_ge(gathered[k], 16 * OWN[k])

        @block.tensor
        def _(pe):
            def turn_rows(n, g, bank_free):
                if n >= 1:
                    pe.wait_ge(bank_free, n)
                for j in range(GROUP):
                    t = nc.tensor.transpose(xt_ps[0:F, j * P:(j + 1) * P], x[:, g * GROUP + j, :], ident[:, :])
                t.then_inc(xt_made, 1)

            def project_rows(n, l, dst=wh_ps):
                pe.wait_ge(xt_copied, n + 1)
                if n >= 1:
                    pe.wait_ge(wh_copied, n)
                for j in range(GROUP):
                    t = nc.tensor.matmul(dst[:, j * WX:(j + 1) * WX], xt[:, n % 2, j * P:(j + 1) * P],
                                         wx[:, l, :], start=True, stop=True)
                t.then_inc(wh_made, 1)

            def sum_rows(l):
                pe.wait_ge(xt_copied, (l + 1) * GROUPS)
                pe.wait_ge(wh_copied, (l + 1) * GROUPS)
                for g in range(GROUPS):
                    t = nc.tensor.matmul(wh_ps[:, 0:F], xsum[:, g:g + 1].broadcast_to([F, P]), wx[:, l, 0:F],
                                         start=(g == 0), stop=(g == GROUPS - 1))
                t.then_inc(sum_made, 1)

            pe.wait_ge(loaded, 16 * NLOAD)
            for l in range(LAYERS):
                if l >= 1:
                    pe.wait_ge(wx_copied, l)
                nc.tensor.transpose(xt_ps[0:F, 0:F], wx[:, l, 0:F], ident[0:F, 0:F]).then_inc(wt_done, 1)
                pe.wait_ge(wt_copied, l + 1)
                nc.tensor.matmul(wh_ps[0:F, 0:2], wt[:, :], wx[:, l, F:WX], start=True, stop=True).then_inc(wa_done, 1)
            pe.wait_ge(wx_copied, LAYERS)
            pe.wait_ge(cast_made, 1)

            def pack(k):
                pe.wait_ge(mask_made, k + 1)
                if k >= CODE_BANKS:
                    pe.wait_ge(codes_read, k - CODE_BANKS + 1)
                codes = codes_ps[k % CODE_BANKS]
                w = WORDS_C + 1
                nc.tensor.matmul(codes[:, 0:TILES * w], ones_b[0:3, :], fix[:, :], start=True, stop=False)
                for c in range(TILES):
                    t = nc.tensor.matmul(codes[:, c * w:(c + 1) * w], masks[:, k % 2, c * P:(c + 1) * P],
                                         packer[:, :], start=False, stop=(c == TILES - 1))
                t.then_inc(codes_made, 1)

            def first_slots(b):
                pe.wait_ge(deg_made, b + 1)
                nc.tensor.matmul(off_ps[:, 0:BATCHES[b][1]], before[:, :], degb[:, 0:BATCHES[b][1]],
                                 start=True, stop=True).then_inc(off_made, 1)

            def lists(b):
                k0, n = BATCHES[b]
                w = ROOM[k0] + 1
                pe.wait_ge(slots_made, k0 + n)
                pe.wait_ge(nbr_made, b + 1)
                for j, (c0, nb) in enumerate(pieces(b)):
                    q = PIECE0[b] + j
                    if q >= 2:
                        pe.wait_ge(list_read, q - 1)
                    for c in range(c0, c0 + nb):
                        tiles = TILES_OF_CHUNK[FIRST[k0] + c]
                        for k in tiles:
                            at = (PLACE[k] - PLACE[k0] + FIRST[k0] + c - FIRST[k]) * P
                            t = nc.tensor.matmul(list_ps[q % 2][:, (c - c0) * w:(c - c0 + 1) * w],
                                                 inrow[:, at:at + P],
                                                 nbrh[:, b % 2, (k - k0) * w:(k - k0 + 1) * w],
                                                 start=(k == tiles[0]), stop=(k == tiles[-1]))
                    t.then_inc(list_made, 1)

            for b in range(len(BATCHES) + 1):
                if b < len(BATCHES):
                    k0, n = BATCHES[b]
                    for k in range(k0, k0 + n):
                        pack(k)
                        if 1 <= k <= GROUPS:
                            project_rows(k - 1, 0)
                        if k == 0:
                            pe.wait_ge(x_loaded, 16)
                        if k < GROUPS:
                            turn_rows(k, k, xt_copied)
                    first_slots(b)
                if b >= 1:
                    lists(b - 1)
            pe.wait_ge(over_made, 1)
            nc.tensor.matmul(off_ps[:, 0:1], ones[:, :], over_sum[:, :], start=True, stop=True).then_inc(over_summed, 1)

            sum_rows(0)

            pe.wait_ge(flag_made, 1)
            over_flag = pe.value_load(flag[0:1, 0:1], min_val=0, max_val=1)
            with pe.If(over_flag == 0):
                def spread(l, q):
                    k, c0, m = SEGS[q]
                    n = l * NSEG + q
                    pe.wait_ge(gathered[k], 16 * OWN[k] * (l + 1))
                    bank = score_ps[n % len(score_ps)]
                    if n >= len(score_ps):
                        pe.wait_ge(masked, n - len(score_ps) + 1)
                    c1 = FIRST[k] + c0
                    at = (PLACE[k] + c0) * P
                    nc.tensor.matmul(bank[:, 0:m * P], ident_b[:, :], penalty[:, at:at + m * P],
                                     start=True, stop=False)
                    for c in range(m):
                        t = nc.tensor.matmul(bank[:, c * P:(c + 1) * P],
                                             tcol_wide(xg[:, c1 + c, TCOL:TCOL + 1]), ident[:, :],
                                             start=False, stop=(c == m - 1))
                    t.then_inc(score_made, 1)

                def turn(l, q):
                    k, c0, m = SEGS[q]
                    n = l * NSEG + q
                    pe.wait_ge(exped, n + 1)
                    if n >= 2:
                        pe.wait_ge(turned_copied, n - 1)
                    for c in range(m):
                        t = nc.tensor.transpose(turned_ps[n % 2][:, c * P:(c + 1) * P],
                                                score[:, n % RING, c * P:(c + 1) * P], ident[:, :])
                    t.then_inc(turned, 1)

                def aggregate(l, q):
                    k, c0, m = SEGS[q]
                    n = l * NSEG + q
                    ng = l * GROUPS + k // GROUP
                    if k % GROUP == 0 and c0 == 0 and ng >= 2:
                        pe.wait_ge(agg_read, ng - 1)
                    pe.wait_ge(turned_copied, n + 1)
                    for c in range(m):
                        t = nc.tensor.matmul(agg_ps[ng % 2][:, (k % GROUP) * F:(k % GROUP + 1) * F],
                                             slots_t[:, n % TRING, c * P:(c + 1) * P],
                                             xg[:, FIRST[k] + c0 + c, 0:F],
                                             start=(c0 + c == 0), stop=(c0 + c == CHUNKS[k] - 1))
                    t.then_inc(aggregated, 1)

                for l in range(LAYERS):
                    if l >= 1:
                        sum_rows(l)
                    for i in range(ROUNDS):
                        g = group_of("project", i)
                        if g is not None and l < LAYERS - 1:
                            if g == 0:
                                pe.wait_ge(sum_copied, l + 1)
                            project_rows((l + 1) * GROUPS + g, l + 1)
                        for q in segs(tile_of("turn", i)):
                            turn(l, q)
                        for q in segs(tile_of("aggregate", i)):
                            aggregate(l, q)
                        g = group_of("turn_x", i)
                        if g is not None and l < LAYERS - 1:
                            pe.wait_ge(x_made, l * GROUPS + g + 1)
                            turn_rows((l + 1) * GROUPS + g, g, xt_copied)
                        for q in segs(tile_of("spread", i)):
                            spread(l, q)
            with pe.Else():
                for l in range(LAYERS):
                    if l > 0:
                        pe.wait_ge(d_x, l * TILES + 1)
                        for g in range(GROUPS):
                            turn_rows(l * GROUPS + g, g, wh_copied)
                            project_rows(l * GROUPS + g, l)
                    pe.wait_ge(wh_copied, (l + 1) * GROUPS)
                    for k in range(TILES):
                        n = l * TILES + k
                        if n >= 2:
                            pe.wait_ge(d_trow_copied, n - 1)
                        nc.tensor.transpose(banks[2 + n % 2][:, 0:P], tcol_wide(wh[:, k, TCOL:TCOL + 1]),
                                            ident[:, :]).then_inc(d_trow, 1)
                    with pe.Fori(0, TILES) as k:
                        pe.wait_ge(d_exp, l * TILES + k + 1)
                        p_f = arena[:, 2, :].bitcast(F32)
                        for c4 in range(TILES // 4):
                            for c in range(4):
                                t = nc.tensor.transpose(turned_ps[0][:, c * P:(c + 1) * P],
                                                        p_f[:, (4 * c4 + c) * P:(4 * c4 + c + 1) * P], ident[:, :])
                            t.then_inc(d_turned, 1)
                            pe.wait_ge(d_turned_copied, (l * TILES + k) * (TILES // 4) + c4 + 1)
                            for c in range(4):
                                t = nc.tensor.matmul(agg_ps[0][:, 0:F], dense_t[:, c * P:(c + 1) * P],
                                                     wh[:, 4 * c4 + c, 0:F],
                                                     start=(c4 + c == 0), stop=(c4 == TILES // 4 - 1 and c == 3))
                            if c4 == TILES // 4 - 1:
                                t.then_inc(d_agg, 1)

        @block.scalar
        def _(sc):
            def copy_wh(n, g, src=wh_ps):
                sc.wait_ge(wh_made, n + 1)
                nc.scalar.copy(wh[:, g * GROUP:(g + 1) * GROUP, :],
                               src[:, 0:GROUP * WX].rearrange("p (j f) -> p j f", j=GROUP)).then_inc(wh_copied, 1)

            def copy_xt(n):
                sc.wait_ge(xt_made, n + 1)
                if n >= 2:
                    sc.wait_ge(wh_made, n - 1)
                nc.scalar.activation(xt[:, n % 2, :], xt_ps[0:F, :], ACT.Copy,
                                     accum_out=xsum[:, n % GROUPS:n % GROUPS + 1]).then_inc(xt_copied, 1)

            def estimate_rstd(h, n, scale, asked, logged, answered, count):
                sc.wait_ge(asked, count)
                nc.scalar.activation(rstd[:, h, 0:n], var[:, h, 0:n], ACT.Ln, scale=scale).then_inc(logged, 1)
                sc.wait_ge(logged, count)
                nc.scalar.activation(rstd[:, h, 0:n], rstd[:, h, 0:n], ACT.Exp, scale=-0.5).then_inc(answered, 1)

            nc.scalar.preload_act_table_set("natural_log_exp_and_others")
            for l in range(LAYERS):
                sc.wait_ge(wt_done, l + 1)
                if l >= 1:
                    sc.wait_ge(wa_done, l)
                nc.scalar.copy(wt[:, :], xt_ps[0:F, 0:F]).then_inc(wt_copied, 1)

            def make_mask(k):
                sc.wait_ge(adj_loaded[k % 3], 16 * (k // 3 + 1))
                if k >= 2:
                    sc.wait_ge(codes_made, k - 1)
                nc.scalar.activation(masks[:, k % 2, :], arena[:, k % 3, :], ACT.Sign, bias=half[:, :]).then_inc(mask_made, 1)

            def slot_signs(b):
                k0, n = BATCHES[b]
                sc.wait_ge(ends_made, b + 1)
                if b == 0:
                    sc.wait_ge(slots_loaded, 32)
                if b >= 1:
                    sc.wait_ge(slots_made, k0)
                for k in range(k0, k0 + n):
                    at = (PLACE[k] - PLACE[k0]) * P
                    w = CHUNKS[k] * P
                    nc.scalar.activation(begun[:, at:at + w], slot_row[:, 0:w], ACT.Sign, bias=from_start[:, k:k + 1])
                    nc.scalar.activation(ended[:, at:at + w], slot_row[:, 0:w], ACT.Sign,
                                         bias=from_end[:, k:k + 1]).then_inc(signed, 1)

            for b in range(len(BATCHES) + 1):
                if b < len(BATCHES):
                    k0, n = BATCHES[b]
                    for k in range(k0, k0 + n):
                        make_mask(k)
                        if 1 <= k <= GROUPS:
                            copy_xt(k - 1)
                        if 2 <= k <= GROUPS + 1:
                            copy_wh(k - 2, k - 2)
                        if k == GROUPS + 1:
                            sc.wait_ge(wh_copied, GROUPS)
                            sc.dma_start(tab_v[0], wh[:, :, :]).then_inc(written, 16)
                if b >= 1:
                    slot_signs(b - 1)

            sc.wait_ge(flag_made, 1)
            over_flag = sc.value_load(flag[0:1, 0:1], min_val=0, max_val=1)
            with sc.If(over_flag == 0):
                def slope(l, q):
                    k, c0, m = SEGS[q]
                    n = l * NSEG + q
                    sc.wait_ge(score_made, n + 1)
                    if n >= RING:
                        sc.wait_ge(turned, n - RING + 1)
                    if k % GROUP == 0 and c0 == 0:
                        sc.wait_ge(slope_made, l * GROUPS + k // GROUP + 1)
                    nc.scalar.activation(score[:, n % RING, 0:m * P], score_ps[n % len(score_ps)][:, 0:m * P], ACT.Relu,
                                         bias=sloped_own[:, k:k + 1], scale=ALPHA[l] - 1.0).then_inc(sloped, 1)

                def exponentials(l, q):
                    k, c0, m = SEGS[q]
                    n = l * NSEG + q
                    sc.wait_ge(max_made, l * TILES + k + 1)
                    s = score[:, n % RING, 0:m * P]
                    nc.scalar.activation(s, s, ACT.Exp, bias=neg_max[:, k:k + 1],
                                         accum_out=seg_sum[:, q:q + 1]).then_inc(exped, 1)

                def copy_turned(l, q):
                    k, c0, m = SEGS[q]
                    n = l * NSEG + q
                    sc.wait_ge(turned, n + 1)
                    if n >= TRING:
                        sc.wait_ge(aggregated, n - TRING + 1)
                    nc.scalar.copy(slots_t[:, n % TRING, 0:m * P], turned_ps[n % 2][:, 0:m * P]).then_inc(turned_copied, 1)

                def elu_part(l, g):
                    sc.wait_ge(agg_read, l * GROUPS + g + 1)
                    nc.scalar.activation(elow[:, g % 2, :, :], num[:, g % 2, :, :], ACT.Exp).then_inc(elow_made, 1)

                for l in range(LAYERS):
                    for i in range(ROUNDS):
                        for q in segs(tile_of("copy_turned", i)):
                            copy_turned(l, q)
                        g = group_of("copy_wh", i)
                        if g is not None and l < LAYERS - 1:
                            copy_wh((l + 1) * GROUPS + g, g)
                        g = group_of("copy_x", i)
                        if g is not None and l < LAYERS - 1:
                            copy_xt((l + 1) * GROUPS + g)
                        for q in segs(tile_of("slope", i)):
                            slope(l, q)
                        g = group_of("rstd", i)
                        if g is not None:
                            estimate_rstd(g % 2, GROUP, -2.0, var_made, ln_made, rstd_made, l * GROUPS + g + 1)
                        g = group_of("elu", i)
                        if g is not None and ELU[l]:
                            elu_part(l, g)
                        for q in segs(tile_of("exp", i)):
                            exponentials(l, q)
            with sc.Else():
                e = 0
                for l in range(LAYERS):
                    if l > 0:
                        for g in range(GROUPS):
                            copy_xt(l * GROUPS + g)
                    for k in range(TILES):
                        n = l * TILES + k
                        sc.wait_ge(d_trow, n + 1)
                        nc.scalar.copy(arena[:, 3, k * P:(k + 1) * P].bitcast(F32),
                                       banks[2 + n % 2][:, 0:P]).then_inc(d_trow_copied, 1)
                    z = arena[:, 2, :].bitcast(F32)
                    sc.wait_ge(d_trow_copied, (l + 1) * TILES)
                    sc.wait_ge(d_slope, l + 1)
                    with sc.Fori(0, TILES) as k:
                        sc.wait_ge(d_x, l * TILES + k + 1)
                        nc.scalar.activation(z, arena[:, 3, :].bitcast(F32), ACT.Identity,
                                             bias=sloped_own[:, bass.ds(k, 1)], scale=ALPHA[l]).then_inc(d_z, 1)
                        sc.wait_ge(d_max, l * TILES + k + 1)
                        nc.scalar.activation(z, arena[:, 1, :].bitcast(F32), ACT.Exp, bias=neg_max[:, 0:1],
                                             accum_out=seg_sum[:, 0:1]).then_inc(d_exp, 1)
                        for c4 in range(TILES // 4):
                            sc.wait_ge(d_turned, (l * TILES + k) * (TILES // 4) + c4 + 1)
                            nc.scalar.copy(dense_t[:, :], turned_ps[0][:, :]).then_inc(d_turned_copied, 1)
                        sc.wait_ge(d_low, l * TILES + k + 1)
                        nc.scalar.activation(elow[:, 0, 0, :], low[:, 0, 0, :], ACT.Exp).then_inc(d_elow, 1)
                        estimate_rstd(0, 1, 1.0, d_var, d_ln, d_rstd, l * TILES + k + 1)

        @block.vector
        def _(v):
            steps = [0]

            def link(ins):
                steps[0] += 1
                ins.then_inc(dve, 1)
                v.wait_ge(dve, steps[0])

            def copy_wh(n, g):
                v.wait_ge(wh_made, n + 1)
                nc.vector.tensor_copy(wh[:, g * GROUP:(g + 1) * GROUP, :],
                                      wh_ps[:, 0:GROUP * WX].rearrange("p (j f) -> p j f", j=GROUP)).then_inc(wh_copied, 1)

            nc.vector.memset(half[:, :], -0.5)
            v.wait_ge(loaded, 16 * NLOAD)
            for dst, src in [(packer, packer_f), (fix, fix_f), (ones_b, ones), (before, before_f), (ident_b, ident)]:
                t = nc.vector.tensor_copy(dst[:, :], src[:, :])
            t.then_inc(cast_made, 1)
            for l in range(LAYERS):
                v.wait_ge(wa_done, l + 1)
                nc.vector.tensor_copy(wx[:, l, TCOL:TCOL + 1], wh_ps[0:F, 1:2])
                nc.vector.tensor_copy(wx[:, l, SCOL:SCOL + 1], wh_ps[0:F, 0:1]).then_inc(wx_copied, 1)
            lane = [(dve, 0)] * max(BMAX, LANES)
            counts = {}

            def ready(j=None):
                for at in set(lane if j is None else [lane[j]]):
                    if at[1] > 0:
                        v.wait_ge(*at)

            def done(ins, j=None, signal=None):
                signal = signal or dve
                if signal is dve:
                    steps[0] += 1
                    count = steps[0]
                else:
                    count = counts[signal] = counts.get(signal, 0) + 1
                ins.then_inc(signal, 1)
                for t in range(len(lane)) if j is None else [j]:
                    lane[t] = (signal, count)

            def first_round(k, j, room):
                v.wait_ge(codes_made, k + 1)
                both = codes_ps[k % CODE_BANKS][:, 0:TILES * (WORDS_C + 1)].rearrange("p (c w) -> p c w", w=WORDS_C + 1)
                parts = SPLIT if room > PART else 1
                each = room // parts
                for t in range(parts):
                    words = both[:, t::parts, 0:WORDS_C]
                    done(nc.vector.max(out=top[:, j * room + t * each:j * room + t * each + 8], in_=words), j + t)
                done(nc.vector.tensor_reduce(deg[:, k:k + 1], both[:, :, WORDS_C], AX, ALU.add), j,
                     codes_read if room == 8 else None)
                if room > 8:
                    for t in range(parts):
                        ready(j + t)
                        done(nc.vector.match_replace(
                            out=key[:, 0, j + t, 0:WORDS // parts].rearrange("p (c w) -> p c w", w=WORDS_C),
                            in_to_replace=top[:, j * room + t * each:j * room + t * each + 8],
                            in_values=both[:, t::parts, 0:WORDS_C], imm_value=0.0), j + t,
                            codes_read if t == parts - 1 else None)

            def top_rounds(n, room, dst, buf, width, first=0):
                cur = 0
                for r in range(first, room // 8):
                    for j in range(n):
                        at = j * room + 8 * r
                        ready(j)
                        done(nc.vector.max(out=dst[:, at:at + 8], in_=buf(cur, j)), j)
                    if r < room // 8 - 1:
                        for j in range(n):
                            at = j * room + 8 * r
                            ready(j)
                            done(nc.vector.match_replace(out=buf(1 - cur, j), in_to_replace=dst[:, at:at + 8],
                                                         in_values=buf(cur, j), imm_value=0.0), j)
                        cur = 1 - cur

            def list_neighbours(b):
                k0, n = BATCHES[b]
                room = ROOM[k0]
                places = n * room
                ready()
                done(nc.vector.tensor_copy(degb[:, 0:n], deg[:, k0:k0 + n]), None, deg_made)
                parts = SPLIT if room > PART else 1
                top_rounds(n * parts, room // parts, top, lambda cur, j: key[:, cur, j, 0:WORDS // parts],
                           WORDS // parts, first=1)
                ready()
                done(nc.vector.tensor_copy(topi[:, 0:places], top[:, 0:places]))
                ready()
                done(nc.vector.tensor_scalar(word[:, 0:places], topi[:, 0:places], WORDS - 1, None,
                                             ALU.bitwise_and), None, word_made)
                wide = [P, places, BITS]
                done(nc.vector.tensor_tensor(bitv[:, 0:places * BITS].rearrange("p (r b) -> p r b", b=BITS),
                                             topi[:, 0:places].unsqueeze(2).broadcast_to(wide),
                                             bit_mask[:, :].unsqueeze(1).broadcast_to(wide), ALU.bitwise_and))
                if b >= 1:
                    pick_neighbours(b - 1)
                v.wait_ge(off_made, b + 1)
                start, end = from_start[:, k0:k0 + n], from_end[:, k0:k0 + n]
                nc.vector.scalar_tensor_tensor(out=start, in0=off_ps[:, 0:n], scalar=-1.0, in1=half_less[:, k0:k0 + n],
                                               op0=ALU.mult, op1=ALU.add).then_inc(starts_made, 1)
                v.wait_ge(starts_made, b + 1)
                nc.vector.tensor_tensor(end, start, deg[:, k0:k0 + n], ALU.subtract).then_inc(ends_made, 1)
                lists_h = nbrh[:, b % 2, 0:n * (room + 1)].rearrange("p (t r) -> p t r", r=room + 1)
                nc.vector.tensor_scalar(lists_h[:, :, room], off_ps[:, 0:n], 0.5, 8.0 * CENTER, ALU.mult, ALU.min)
                ready()
                v.wait_ge(col_made, b + 1)
                done(nc.vector.scalar_tensor_tensor(out=cand[:, 0, 0:places * BITS], in0=bitv[:, 0:places * BITS],
                                                    scalar=0.0, in1=colv[:, 0:places * BITS], op0=ALU.is_gt,
                                                    op1=ALU.mult), None, col_used)
                if room > PART:
                    w = PART * BITS
                    parts = room // PART
                    top_rounds(parts, PART_ROOM, found[:, 0, :], lambda cur, j: cand[:, cur, j * w:(j + 1) * w], w)
                    ready()
                    top_rounds(1, room, nbr, lambda cur, j: found[:, cur, 0:parts * PART_ROOM], parts * PART_ROOM)
                    ready()
                    done(nc.vector.tensor_scalar(found[:, 0, 0:room], nbr[:, 0:room], 0.0, None, ALU.is_gt))
                    ready()
                    done(nc.vector.tensor_reduce(limits[:, 0, k0:k0 + 1], found[:, 0, 0:room], AX, ALU.add))
                else:
                    w = room * BITS
                    top_rounds(n, room, nbr, lambda cur, j: cand[:, cur, j * w:(j + 1) * w], w)
                ready()
                done(nc.vector.tensor_scalar(lists_h[:, :, 0:room], nbr[:, 0:places].rearrange("p (t r) -> p t r", r=room),
                                             float(-1 - CENTER), 0.5, ALU.add, ALU.mult), None, nbr_made)

            def pick_neighbours(b):
                k0, n = BATCHES[b]
                room = ROOM[k0]
                v.wait_ge(slots_made, k0 + n)
                nc.vector.tensor_scalar(penalty[:, PLACE[k0] * P:PLACE[k0 + n] * P],
                                        inrow[:, 0:(PLACE[k0 + n] - PLACE[k0]) * P], 2.0, -MASKED / 2,
                                        ALU.subtract, ALU.mult).then_inc(penalty_made, 1)
                for i, (c0, nb) in enumerate(pieces(b)):
                    q = PIECE0[b] + i
                    h = q % 2
                    c1 = FIRST[k0] + c0
                    v.wait_ge(list_made, q + 1)
                    lists = list_ps[h][:, 0:nb * (room + 1)].rearrange("p (c r) -> p c r", r=room + 1)
                    shape = [P, nb, room]
                    pk = pick[:, h, 0:nb * room].rearrange("p (c r) -> p c r", r=room)
                    rk = rank[:, h, 0:nb]
                    link(nc.vector.tensor_tensor(rk, slot_col[:, c1:c1 + nb], lists[:, :, room], ALU.subtract))
                    link(nc.vector.tensor_tensor(pk, room_row[:, 0:room].unsqueeze(1).broadcast_to(shape),
                                                 rk.unsqueeze(2).broadcast_to(shape), ALU.is_equal))
                    nc.vector.tensor_tensor(pk, pk, lists[:, :, 0:room], ALU.mult).then_inc(list_read, 1)
                    v.wait_ge(list_read, q + 1)
                    link(nc.vector.tensor_reduce(picked[:, h, 0:nb], pk, AX, ALU.add))
                    link(nc.vector.tensor_scalar(picked[:, h, 0:nb], picked[:, h, 0:nb], -float(CENTER), CENTER - 1.0,
                                                 ALU.max, ALU.min))
                    t = nc.vector.tensor_scalar(index[:, c1:c1 + nb], picked[:, h, 0:nb], float(CENTER), None, ALU.add)
                t.then_inc(index_made, 1)

            for b, (k0, n) in enumerate(BATCHES):
                for k in range(k0, k0 + n):
                    first_round(k, k - k0, ROOM[k0])
                list_neighbours(b)
            pick_neighbours(len(BATCHES) - 1)
            ready()
            link(nc.vector.tensor_scalar(lonely[:, :], deg[:, :], 0.0, None, ALU.is_equal))
            link(nc.vector.tensor_tensor(over[:, 0, :], deg[:, :], limits[:, 0, :], ALU.is_gt))
            link(nc.vector.tensor_tensor(over[:, 1, :], from_end[:, :], limits[:, 1, :], ALU.is_lt))
            nc.vector.tensor_reduce(over_sum[:, :], over[:, :, :].rearrange("p a b -> p (a b)"), AX,
                                    ALU.add).then_inc(over_made, 1)
            v.wait_ge(over_summed, 1)
            nc.vector.tensor_scalar(flag[0:1, 0:1], off_ps[0:1, 0:1], 0.0, None, ALU.is_gt).then_inc(flag_made, 1)
            v.wait_ge(flag_made, 1)

            over_flag = v.value_load(flag[0:1, 0:1], min_val=0, max_val=1)

            def center(link, h, n, asked):
                wide = [P, n, F]
                y, st, sq = res[:, h, 0:n, :], stat[:, h, 0:n], num[:, h, 0:n, :]
                link(nc.vector.tensor_reduce(st, y, AX, ALU.add))
                link(nc.vector.tensor_scalar(st, st, -1.0 / F, None, ALU.mult))
                link(nc.vector.tensor_tensor(y, y, st.unsqueeze(2).broadcast_to(wide), ALU.add))
                link(nc.vector.tensor_tensor(sq, y, y, ALU.mult))
                link(nc.vector.tensor_reduce(st, sq, AX, ALU.add))
                nc.vector.tensor_scalar(var[:, h, 0:n], st, 1.0 / F, EPS, ALU.mult, ALU.add).then_inc(asked, 1)

            def scale_rows(link, h, n, xs, answered, count, last):
                y, st, r, va = res[:, h, 0:n, :], stat[:, h, 0:n], rstd[:, h, 0:n], var[:, h, 0:n]
                v.wait_ge(answered, count)
                link(nc.vector.tensor_tensor(st, r, r, ALU.mult))
                link(nc.vector.tensor_tensor(st, st, va, ALU.mult))
                link(nc.vector.tensor_scalar(st, st, -0.5, 1.5, ALU.mult, ALU.add))
                link(nc.vector.tensor_tensor(st, st, r, ALU.mult))
                last(nc.vector.tensor_tensor(xs, y, st.unsqueeze(2).broadcast_to([P, n, F]), ALU.mult))

            with v.If(over_flag == 0):
                def slope(l, g):
                    k = g * GROUP
                    nc.vector.tensor_scalar(sloped_own[:, k:k + GROUP], wh[:, k:k + GROUP, SCOL], ALPHA[l] - 1.0, None,
                                            ALU.mult).then_inc(slope_made, 1)

                def mask_scores(l, k):
                    for q in segs(k):
                        _, c0, m = SEGS[q]
                        n = l * NSEG + q
                        y = score[:, n % RING, 0:m * P]
                        v.wait_ge(sloped, n + 1)
                        nc.vector.tensor_tensor_reduce(out=y, in0=score_ps[n % len(score_ps)][:, 0:m * P], in1=y, scale=1.0,
                                                       scalar=MASKED, op0=ALU.add, op1=ALU.max,
                                                       accum_out=seg_max[:, q:q + 1]).then_inc(masked, 1)
                    q = SEG0[k]
                    v.wait_ge(masked, l * NSEG + q + SEGN[k])
                    rm = seg_max[:, q:q + 1]
                    if SEGN[k] > 1:
                        rm = row_max[:, k:k + 1]
                        link(nc.vector.tensor_reduce(rm, seg_max[:, q:q + SEGN[k]], AX, ALU.max))
                    nc.vector.tensor_scalar(neg_max[:, k:k + 1], rm, FLOOR, -1.0, ALU.max, ALU.mult).then_inc(max_made, 1)

                def combine(l, g):
                    k0, h = g * GROUP, g % 2
                    y = num[:, h, :, :]
                    v.wait_ge(aggregated, l * NSEG + GROUP_END[g])
                    several = max(SEGN[k0:k0 + GROUP]) > 1
                    if several:
                        for j in range(GROUP):
                            q, n = SEG0[k0 + j], SEGN[k0 + j]
                            t = nc.vector.tensor_reduce(den[:, j:j + 1], seg_sum[:, q:q + n], AX, ALU.add)
                        link(t)
                    src = den[:, :] if several else seg_sum[:, SEG0[k0]:SEG0[k0] + GROUP]
                    link(nc.vector.tensor_tensor(den[:, :], src, lonely[:, k0:k0 + GROUP], ALU.add))
                    link(nc.vector.reciprocal(den[:, :], den[:, :]))
                    for j in range(GROUP):
                        t = nc.vector.scalar_tensor_tensor(
                            out=y[:, j, :], in0=agg_ps[(l * GROUPS + g) % 2][:, j * F:(j + 1) * F],
                            scalar=den[:, j:j + 1], in1=lone_rows[:, k0 + j, :], op0=ALU.mult, op1=ALU.add)
                    t.then_inc(agg_read, 1)
                    v.wait_ge(agg_read, l * GROUPS + g + 1)
                    xs = x[:, k0:k0 + GROUP, :]
                    if l == BIAS_LAYER:
                        link(nc.vector.tensor_tensor(y, y, bias_sb[:, :].unsqueeze(1).broadcast_to([P, GROUP, F]), ALU.add))
                    if ELU[l]:
                        nc.vector.scalar_tensor_tensor(out=res[:, h, :, :], in0=y, scalar=0.0, in1=xs,
                                                       op0=ALU.max, op1=ALU.add).then_inc(res_made, 1)
                    else:
                        nc.vector.tensor_tensor(res[:, h, :, :], y, xs, ALU.add).then_inc(res_made, 1)

                def norm_stats(l, g):
                    h = g % 2
                    y = res[:, h, :, :]
                    v.wait_ge(res_made, l * GROUPS + g + 1)
                    if ELU[l]:
                        v.wait_ge(elow_made, sum(ELU[:l]) * GROUPS + g + 1)
                        link(nc.vector.scalar_tensor_tensor(out=y, in0=elow[:, h, :, :], scalar=1.0, in1=y,
                                                            op0=ALU.min, op1=ALU.add))
                    for j in range(GROUP):
                        t = nc.vector.bn_stats(out=stats[:, j, :], in_=y[:, j, :])
                    link(t)
                    for j in range(GROUP):
                        t = nc.vector.bn_aggr(out=mean_var[:, h, j, :], in_=stats[:, j, :])
                    link(t)
                    nc.vector.tensor_scalar(var[:, h, :], mean_var[:, h, :, 1], -0.5, -0.5 * EPS, ALU.mult,
                                            ALU.add).then_inc(var_made, 1)
                    nc.vector.tensor_tensor(y, y, mean_var[:, h, :, 0].unsqueeze(2).broadcast_to([P, GROUP, F]),
                                            ALU.subtract).then_inc(centered, 1)

                def norm_rows(l, g):
                    h = g % 2
                    st, r = stat[:, h, :], rstd[:, h, :]
                    v.wait_ge(rstd_made, l * GROUPS + g + 1)
                    link(nc.vector.tensor_tensor(st, r, r, ALU.mult))
                    link(nc.vector.tensor_tensor(st, st, var[:, h, :], ALU.mult))
                    link(nc.vector.scalar_tensor_tensor(out=st, in0=st, scalar=1.5, in1=r, op0=ALU.add, op1=ALU.mult))
                    v.wait_ge(centered, l * GROUPS + g + 1)
                    nc.vector.tensor_tensor(x[:, g * GROUP:(g + 1) * GROUP, :], res[:, h, :, :],
                                            st.unsqueeze(2).broadcast_to([P, GROUP, F]), ALU.mult).then_inc(x_made, 1)

                for l in range(LAYERS):
                    for i in range(ROUNDS):
                        if l == 0 and i == 0:
                            v.wait_ge(wh_copied, GROUPS)
                            for g in range(GROUPS):
                                slope(0, g)
                        if i == 0:
                            v.wait_ge(sum_made, l + 1)
                            nc.vector.tensor_scalar(sum_wh[:, :], wh_ps[:, 0:F], 1.0 / N, None,
                                                    ALU.mult).then_inc(sum_copied, 1)
                            v.wait_ge(sum_copied, l + 1)
                            link(nc.vector.tensor_tensor(lone_rows[:, :, :],
                                                         sum_wh[:, :].unsqueeze(1).broadcast_to([P, TILES, F]),
                                                         lonely[:, :].unsqueeze(2).broadcast_to([P, TILES, F]), ALU.mult))
                        k = tile_of("mask", i)
                        if k is not None:
                            mask_scores(l, k)
                        g = group_of("combine", i)
                        if g is not None:
                            combine(l, g)
                        g = group_of("scale", i)
                        if g is not None:
                            norm_rows(l, g)
                        g = group_of("center", i)
                        if g is not None:
                            norm_stats(l, g)
                        g = group_of("own", i)
                        if g is not None and l < LAYERS - 1:
                            v.wait_ge(wh_copied, (l + 1) * GROUPS + g + 1)
                            slope(l + 1, g)
            with v.Else():
                nc.vector.memset(stat[:, 0, 0:1], 0.0).then_inc(d_x, 1)
                v.wait_ge(d_x, 1)
                for l in range(LAYERS):
                    if l > 0:
                        for g in range(GROUPS):
                            copy_wh(l * GROUPS + g, g)
                    v.wait_ge(wh_copied, (l + 1) * GROUPS)
                    nc.vector.tensor_scalar(sloped_own[:, :], wh[:, :, SCOL], ALPHA[l], None, ALU.mult).then_inc(d_slope, 1)
                    own = wh[:, :, SCOL]
                    trow = arena[:, 3, :].bitcast(F32)
                    adj_sb, pen, z = arena[:, 0, :], arena[:, 1, :].bitcast(F32), arena[:, 2, :].bitcast(F32)
                    per = 21
                    with v.Fori(0, TILES) as k:
                        n = [0]

                        def dlink(ins):
                            n[0] += 1
                            ins.then_inc(d_dve, 1)
                            v.wait_ge(d_dve, (l * TILES + k) * per + n[0])
                        v.wait_ge(d_adj, (l * TILES + k + 1) * 16)
                        dlink(nc.vector.tensor_scalar(pen, adj_sb, 0, MASKED, ALU.is_le, ALU.mult))
                        v.wait_ge(d_z, l * TILES + k + 1)
                        dlink(nc.vector.scalar_tensor_tensor(out=z, in0=trow, scalar=own[:, bass.ds(k, 1)], in1=z,
                                                             op0=ALU.add, op1=ALU.max))
                        dlink(nc.vector.tensor_tensor(pen, pen, z, ALU.add))
                        dlink(nc.vector.tensor_reduce(row_max[:, 0:1], pen, AX, ALU.max))
                        nc.vector.tensor_scalar(neg_max[:, 0:1], row_max[:, 0:1], -1.0, None, ALU.mult).then_inc(d_max, 1)
                        v.wait_ge(d_agg, l * TILES + k + 1)
                        dlink(nc.vector.reciprocal(den[:, 0:1], seg_sum[:, 0:1]))
                        dlink(nc.vector.tensor_scalar(num[:, 0, 0, :], agg_ps[0][:, 0:F], den[:, 0:1], None, ALU.mult))
                        xs = x[:, bass.ds(k, 1), :]
                        if l == BIAS_LAYER:
                            dlink(nc.vector.tensor_tensor(num[:, 0, 0, :], num[:, 0, 0, :], bias_sb[:, :], ALU.add))
                        nc.vector.tensor_scalar(low[:, 0, 0, :], num[:, 0, 0, :], 0.0, None, ALU.min).then_inc(d_low, 1)
                        if ELU[l]:
                            dlink(nc.vector.scalar_tensor_tensor(out=res[:, 0, 0:1, :], in0=num[:, 0, 0:1, :], scalar=0.0, in1=xs,
                                                                 op0=ALU.max, op1=ALU.add))
                            v.wait_ge(d_elow, l * TILES + k + 1)
                            dlink(nc.vector.scalar_tensor_tensor(out=res[:, 0, 0:1, :], in0=elow[:, 0, 0:1, :], scalar=-1.0,
                                                                 in1=res[:, 0, 0:1, :], op0=ALU.add, op1=ALU.add))
                        else:
                            dlink(nc.vector.tensor_tensor(res[:, 0, 0:1, :], num[:, 0, 0:1, :], xs, ALU.add))
                            v.wait_ge(d_elow, l * TILES + k + 1)

                        def last(ins):
                            ins.then_inc(d_x, 1)
                            v.wait_ge(d_x, l * TILES + k + 2)
                        center(dlink, 0, 1, d_var)
                        scale_rows(dlink, 0, 1, xs, d_rstd, l * TILES + k + 1, last)
                        while n[0] < per:
                            dlink(nc.vector.tensor_copy(stat[:, 0, 0:1], den[:, 0:1]))


def _constants():
    p = np.arange(P)
    packer = np.zeros((P, WORDS_C + 1), np.float32)
    packer[p, p % WORDS_C] = WORDS * 2.0 ** (p // WORDS_C) / 2
    packer[:, WORDS_C] = 0.5
    fix = np.zeros((3, TILES, WORDS_C + 1), np.float32)
    fix[0, :, 0:WORDS_C] = WORDS * 2.0 ** BITS / 2
    fix[1, :, 0:WORDS_C] = -WORDS / 2
    fix[2, :, 0:WORDS_C] = np.arange(WORDS).reshape(WORDS_C, TILES).T
    fix[0, :, WORDS_C] = P / 2
    slot = np.concatenate([np.arange(u * UNIT) for u in UNITS]).reshape(NCH, P).T

    def rows(a):
        return np.broadcast_to(np.asarray(a), (P, len(a)))
    packed = [np.eye(P), np.ones((P, P)), p[:, None] < p[None, :], packer, slot,
              rows(np.arange(MAXR)), rows(WORDS * np.arange(BITS) + 1), rows([0.5 - o for o in OFFSET]),
              rows(ROOM + [-(OFFSET[k] + UNITS[k] * UNIT) for k in range(TILES)])]
    return {
        "packed": np.concatenate([a.astype(np.float32) for a in packed], axis=1),
        "fix": fix.reshape(3, -1),
        "slot_row": rows(np.arange(MAXC * P)).astype(np.float32),
        "bit_mask": rows(WORDS << np.arange(BITS)).astype(np.int32),
    }


def kernel(x, adj, L0_gnn_W, L0_gnn_a, L1_gnn_weight_w, L1_gnn_weight_a, L1_gnn_bias,
           L2_gnn_W, L2_gnn_a, L3_gnn_W, L3_gnn_a):
    import numpy as _np
    import concourse.bacc as _bacc
    from concourse import mybir as _mybir
    from concourse.bass_utils import run_bass_kernel_spmd as _run

    adj = _np.asarray(adj)
    adj_t = adj.reshape(TILES, P, TILES, P).transpose(0, 3, 2, 1).reshape(TILES, P, N)
    layers = [(L0_gnn_W, L0_gnn_a), (L1_gnn_weight_w, L1_gnn_weight_a), (L2_gnn_W, L2_gnn_a), (L3_gnn_W, L3_gnn_a)]
    weights = _np.stack([_np.concatenate([_np.asarray(w), _np.asarray(a).reshape(2, F).T], axis=1) for w, a in layers],
                        axis=1)
    feeds = {"x": _np.asarray(x).reshape(TILES, P, F).transpose(1, 0, 2), "adj": adj, "adj_t": adj_t,
             "weights": weights, "bias": L1_gnn_bias}
    feeds.update({f"c_{n}": a for n, a in _constants().items()})

    nc = _bacc.Bacc("TRN2", target_bir_lowering=False, num_devices=1)
    arrays, aps = {}, {}
    for name, a in feeds.items():
        a = _np.ascontiguousarray(a)
        arrays[f"in_{name}"] = a
        aps[name] = nc.dram_tensor(f"in_{name}", a.shape, _mybir.dt.from_np(a.dtype), kind="ExternalInput").ap()
    out = nc.dram_tensor("out_x", (P, TILES, F), _mybir.dt.float32, kind="ExternalOutput").ap()
    gat_kernel(nc, aps["x"], aps["adj"], aps["adj_t"], aps["weights"], aps["bias"],
               {n[2:]: a for n, a in aps.items() if n.startswith("c_")}, out)
    out_x = _run(nc, [arrays], core_ids=[0]).results[0]["out_x"]
    return _np.asarray(out_x).reshape(P, TILES, F).transpose(1, 0, 2).reshape(N, F)
```
